# Optimizing a Trainium2 kernel written in Bass

```python
import numpy as np
import jax
import jax.numpy as jnp

def _softmax(x, axis=-1):
    return jax.nn.softmax(x, axis=axis)

def _gelu(x):
    return jax.nn.gelu(x, approximate=True)

def _silu(x):
    return jax.nn.silu(x)

def _sigmoid(x):
    return jax.nn.sigmoid(x)

def _layernorm(x, axis=-1, eps=1e-05):
    m = jnp.mean(x, axis=axis, keepdims=True)
    v = jnp.var(x, axis=axis, keepdims=True)
    return (x - m) / jnp.sqrt(v + eps)

def _scatter_add(tgt, idx, src, axis=0):
    return tgt.at[idx].add(src)

def _segment_sum(src, seg, n):
    return jax.ops.segment_sum(src, seg, n)
kernel_name = 'mk_adaln_d1_jaxref_r8_e23a3e'

def setup_inputs(seed: int=0):
    np.random.seed(seed)
    _w = jnp.asarray

    def _L0_attn_setup():
        import jax, jax.numpy as jnp
        import numpy as np
        HID = 128
        EXP = 512

        def _min_gru(x_in, Wz, bz, Wh, bh):
            z = jax.nn.sigmoid(jnp.einsum('bse,ef->bsf', x_in, Wz) + bz)
            h_tilde = jnp.einsum('bse,ef->bsf', x_in, Wh) + bh
            a = 1.0 - z
            b = z * h_tilde

            def combine(c1, c2):
                a1, b1 = c1
                a2, b2 = c2
                return (a2 * a1, a2 * b1 + b2)
            _, h = jax.lax.associative_scan(combine, (a, b), axis=1)
            return h
        key = jax.random.key(seed)
        ks = jax.random.split(key, 11)
        s = lambda fan_in: 1.0 / np.sqrt(fan_in)
        return {'x': jax.random.normal(ks[0], (4, 256, HID), dtype=jnp.float32), 'W1': jax.random.uniform(ks[1], (HID, EXP), jnp.float32, -s(HID), s(HID)), 'b1': jax.random.uniform(ks[2], (EXP,), jnp.float32, -s(HID), s(HID)), 'W2': jax.random.uniform(ks[3], (HID, EXP), jnp.float32, -s(HID), s(HID)), 'b2': jax.random.uniform(ks[4], (EXP,), jnp.float32, -s(HID), s(HID)), 'Wz': jax.random.uniform(ks[5], (EXP, EXP), jnp.float32, -s(EXP), s(EXP)), 'bz': jax.random.uniform(ks[6], (EXP,), jnp.float32, -s(EXP), s(EXP)), 'Wh': jax.random.uniform(ks[7], (EXP, EXP), jnp.float32, -s(EXP), s(EXP)), 'bh': jax.random.uniform(ks[8], (EXP,), jnp.float32, -s(EXP), s(EXP)), 'Wo': jax.random.uniform(ks[9], (EXP, HID), jnp.float32, -s(EXP), s(EXP)), 'bo': jax.random.uniform(ks[10], (HID,), jnp.float32, -s(EXP), s(EXP))}
    _L0_attn_in = _L0_attn_setup()

    def _L0_ffn_setup():
        import jax, jax.numpy as jnp
        import numpy as np
        MICRO_BATCHES = 2
        TOP_K = 2
        LN_EPS = 1e-05
        B, S, D = (4, 512, 128)
        E = 8
        DFF = 4 * D

        def _layernorm(x, g, b):
            mu = jnp.mean(x, axis=-1, keepdims=True)
            var = jnp.mean(jnp.square(x - mu), axis=-1, keepdims=True)
            return (x - mu) * jax.lax.rsqrt(var + LN_EPS) * g + b
        key = jax.random.key(seed)
        ks = jax.random.split(key, 12)
        sd = 1.0 / np.sqrt(D)
        sf = 1.0 / np.sqrt(DFF)
        return {'x': jax.random.normal(ks[0], (B, S, D), dtype=jnp.float32), 'ln_g': jnp.ones((D,), jnp.float32), 'ln_b': jnp.zeros((D,), jnp.float32), 'attn_w': jax.random.normal(ks[1], (D, D), jnp.float32) * sd, 'attn_b': jnp.zeros((D,), jnp.float32), 'gate_w': jax.random.normal(ks[2], (D, E), jnp.float32) * sd, 'w1': jax.random.normal(ks[3], (E, D, DFF), jnp.float32) * sd, 'b1': jnp.zeros((E, DFF), jnp.float32), 'w2': jax.random.normal(ks[4], (E, DFF, D), jnp.float32) * sf, 'b2': jnp.zeros((E, D), jnp.float32), 'next_w': jax.random.normal(ks[5], (D, D), jnp.float32) * sd, 'next_b': jnp.zeros((D,), jnp.float32)}
    _L0_ffn_in = _L0_ffn_setup()
    _L0_c = _w((lambda *s: np.random.randn(*s).astype(np.float32) * 0.05)(4, 128))
    _L0_wmod = _w((lambda *s: np.random.randn(*s).astype(np.float32) * 0.05)(128, 6 * 128) * 128 ** (-0.5))
    _d = {'L0_attn_x': _L0_attn_in['x'], 'L0_attn_W1': _L0_attn_in['W1'], 'L0_attn_b1': _L0_attn_in['b1'], 'L0_attn_W2': _L0_attn_in['W2'], 'L0_attn_b2': _L0_attn_in['b2'], 'L0_attn_Wz': _L0_attn_in['Wz'], 'L0_attn_bz': _L0_attn_in['bz'], 'L0_attn_Wh': _L0_attn_in['Wh'], 'L0_attn_bh': _L0_attn_in['bh'], 'L0_attn_Wo': _L0_attn_in['Wo'], 'L0_attn_bo': _L0_attn_in['bo'], 'L0_ffn_ln_g': _L0_ffn_in['ln_g'], 'L0_ffn_ln_b': _L0_ffn_in['ln_b'], 'L0_ffn_attn_w': _L0_ffn_in['attn_w'], 'L0_ffn_attn_b': _L0_ffn_in['attn_b'], 'L0_ffn_gate_w': _L0_ffn_in['gate_w'], 'L0_ffn_w1': _L0_ffn_in['w1'], 'L0_ffn_b1': _L0_ffn_in['b1'], 'L0_ffn_w2': _L0_ffn_in['w2'], 'L0_ffn_b2': _L0_ffn_in['b2'], 'L0_ffn_next_w': _L0_ffn_in['next_w'], 'L0_ffn_next_b': _L0_ffn_in['next_b'], 'L0_c': _L0_c, 'L0_wmod': _L0_wmod}
    _x0 = _d['L0_attn_x']
    _d['L0_attn_x'] = jax.random.normal(jax.random.fold_in(jax.random.key(seed), 1), (4, 1024, 128), dtype=_x0.dtype)
    del _x0
    return _d

def reference(L0_attn_x, L0_attn_W1, L0_attn_b1, L0_attn_W2, L0_attn_b2, L0_attn_Wz, L0_attn_bz, L0_attn_Wh, L0_attn_bh, L0_attn_Wo, L0_attn_bo, L0_ffn_ln_g, L0_ffn_ln_b, L0_ffn_attn_w, L0_ffn_attn_b, L0_ffn_gate_w, L0_ffn_w1, L0_ffn_b1, L0_ffn_w2, L0_ffn_b2, L0_ffn_next_w, L0_ffn_next_b, L0_c, L0_wmod):

    def _L0_attn_ref(x, W1, b1, W2, b2, Wz, bz, Wh, bh, Wo, bo):
        import jax, jax.numpy as jnp
        import numpy as np
        HID = 128
        EXP = 512

        def _min_gru(x_in, Wz, bz, Wh, bh):
            z = jax.nn.sigmoid(jnp.einsum('bse,ef->bsf', x_in, Wz) + bz)
            h_tilde = jnp.einsum('bse,ef->bsf', x_in, Wh) + bh
            a = 1.0 - z
            b = z * h_tilde

            def combine(c1, c2):
                a1, b1 = c1
                a2, b2 = c2
                return (a2 * a1, a2 * b1 + b2)
            _, h = jax.lax.associative_scan(combine, (a, b), axis=1)
            return h
        x_in = jax.nn.silu(jnp.einsum('bsd,de->bse', x, W1) + b1)
        x_skip = jax.nn.silu(jnp.einsum('bsd,de->bse', x, W2) + b2)
        h = _min_gru(x_in, Wz, bz, Wh, bh)
        return jnp.einsum('bse,ed->bsd', x_skip + h, Wo) + bo

    def _L0_ffn_ref(x, ln_g, ln_b, attn_w, attn_b, gate_w, w1, b1, w2, b2, next_w, next_b):
        import jax, jax.numpy as jnp
        import numpy as np
        MICRO_BATCHES = 2
        TOP_K = 2
        LN_EPS = 1e-05
        B, S, D = (4, 512, 128)
        E = 8
        DFF = 4 * D

        def _layernorm(x, g, b):
            mu = jnp.mean(x, axis=-1, keepdims=True)
            var = jnp.mean(jnp.square(x - mu), axis=-1, keepdims=True)
            return (x - mu) * jax.lax.rsqrt(var + LN_EPS) * g + b
        Bx, Sx, Dx = x.shape
        N = Bx * Sx
        x_flat = x.reshape(N, Dx)
        x_attn = _layernorm(x_flat, ln_g, ln_b) @ attn_w + attn_b + x_flat
        logits = x_attn @ gate_w
        _ = jax.lax.top_k(logits, TOP_K)
        tpe = N // (MICRO_BATCHES * E)
        g = x_attn.reshape(MICRO_BATCHES, E, tpe, Dx)
        h = jax.nn.gelu(jnp.einsum('metd,edf->metf', g, w1) + b1[None, :, None, :], approximate=False)
        y = jnp.einsum('metf,efd->metd', h, w2) + b2[None, :, None, :]
        out = jax.nn.gelu(y @ next_w + next_b, approximate=False)
        return out.reshape(Bx, Sx, Dx)
    x = L0_attn_x
    mod = (_silu(L0_c) @ L0_wmod).reshape(L0_c.shape[0], 6, 1, -1)
    sa, ca, ga, sb, cb, gb = (mod[:, 0], mod[:, 1], mod[:, 2], mod[:, 3], mod[:, 4], mod[:, 5])
    ga = (2 * (ga >= 0) - 1) * jnp.maximum(jnp.abs(ga), 0.25)
    gb = (2 * (gb >= 0) - 1) * jnp.maximum(jnp.abs(gb), 0.25)
    h = _layernorm(x, axis=-1) * (1 + ca) + sa
    x = x + ga * _L0_attn_ref(h, L0_attn_W1, L0_attn_b1, L0_attn_W2, L0_attn_b2, L0_attn_Wz, L0_attn_bz, L0_attn_Wh, L0_attn_bh, L0_attn_Wo, L0_attn_bo)
    h = _layernorm(x, axis=-1) * (1 + cb) + sb
    x = x + gb * _L0_ffn_ref(h, L0_ffn_ln_g, L0_ffn_ln_b, L0_ffn_attn_w, L0_ffn_attn_b, L0_ffn_gate_w, L0_ffn_w1, L0_ffn_b1, L0_ffn_w2, L0_ffn_b2, L0_ffn_next_w, L0_ffn_next_b)
    return x

_drawn_inputs = setup_inputs


def setup_inputs(seed=0):
    import zlib

    import numpy as np

    out = dict(_drawn_inputs(seed))
    spreads = {'L0_ffn_ln_g': (1.0, 0.6),
     'L0_ffn_ln_b': (0.0, 0.671),
     'L0_ffn_attn_b': (0.0, 0.724),
     'L0_ffn_b1': (0.0, 0.682),
     'L0_ffn_b2': (0.0, 0.487),
     'L0_ffn_next_b': (0.0, 0.449)}
    factors = {'L0_attn_W1': 3.833,
     'L0_attn_b1': 8.0,
     'L0_attn_b2': 8.0,
     'L0_attn_Wz': 8.0,
     'L0_attn_bz': 35.841,
     'L0_attn_Wh': 3.456,
     'L0_attn_bh': 8.0,
     'L0_attn_bo': 7.965}
    for name, (base, spread) in spreads.items():
        noise = np.random.default_rng([zlib.crc32(name.encode()), seed]).standard_normal(out[name].shape)
        drawn = base * np.exp(spread * noise) if base else spread * noise
        out[name] = jnp.asarray(drawn.astype(out[name].dtype))
    for name, factor in factors.items():
        out[name] = (out[name] * factor).astype(out[name].dtype)
    return out
```

```python
from contextlib import ExitStack

import concourse.bass as bass
from concourse import mybir

F32 = mybir.dt.float32
F16 = mybir.dt.float16
ALU = mybir.AluOpType
ACT = mybir.ActivationFunctionType

P = 128
WSCALE = 64.0
UNSCALE = 1.0 / WSCALE
EPS = 1e-5


def adaln_mingru_experts(nc, x, W1, b1, W2, b2, Wz, bz, Wh, bh, Wo, bo, ln_g, ln_b, attn_w, attn_b,
                         ew1, eb1, ew2, eb2, next_w, next_b, cond, wmod, out):
    B, S, D = x.shape
    EXP = W1.shape[1]
    E = ew1.shape[0]
    J = EXP // P
    HALVES = 2
    CHUNKS = E
    SPAN = B * S // (HALVES * CHUNKS)
    TILES = HALVES * SPAN // P
    N = HALVES * SPAN
    PER_SEQ = S // SPAN
    assert D == P and N == 512 and ew1.shape[2] == EXP and CHUNKS % PER_SEQ == 0 and B == 4

    R_B1, R_B2, R_BZ, R_BH = 0, J, 2 * J, 3 * J
    R_BO = 4 * J
    R_G, R_LB, R_AB, R_NB = R_BO + 1, R_BO + 2, R_BO + 3, R_BO + 4
    R_EB2 = R_BO + 5
    R_EB1 = R_EB2 + E
    R_C = R_EB1 + E * J
    ROWS = R_C + B
    T_SCALE1, T_SHIFT1, T_GATE1, T_GATE1_BO, T_GATE2 = range(5)
    TABLES = 5

    def rows(v):
        return v.rearrange("(a n) -> a n", n=P)

    def token_rows(t):
        return t.rearrange("b s d -> (b s) d").rearrange("(h k t p) d -> h k p t d", h=HALVES, k=CHUNKS, p=P)

    x_rows, out_rows = token_rows(x), token_rows(out)

    with ExitStack() as ctx:
        def sb(name, shape, dt=F32):
            return ctx.enter_context(nc.sbuf_tensor(name, shape, dt))

        def sem(name):
            return ctx.enter_context(nc.semaphore(name))

        def bank(name):
            return ctx.enter_context(nc.psum_tensor(name, [P, N], F32))

        bank_A = [bank("bank_A0"), bank("bank_A1")]
        bank_B = [bank("bank_B0"), bank("bank_B1")]
        bank_C = [bank("bank_C0"), bank("bank_C1")]
        bank_D = bank("bank_D")
        bank_E = bank("bank_E")

        x_all = sb("x_all", [P, CHUNKS, TILES, D])
        n1 = sb("n1", [P, TILES, D])
        u2 = sb("u2", [P, TILES, D])
        h2 = sb("h2", [P, TILES, D])
        n3 = sb("n3", [P, TILES, D])
        stats = {n: sb(f"stats{n}", [P, TILES, 6]) for n in (1, 2, 3)}
        mean_var = {n: sb(f"mean_var{n}", [P, TILES, 2]) for n in (1, 2, 3)}
        var_eps = {n: sb(f"var_eps{n}", [P, TILES]) for n in (1, 2, 3)}
        rstd = {n: sb(f"rstd{n}", [P, TILES]) for n in (1, 2, 3)}
        minus_half = sb("minus_half", [P, TILES])

        xm, xm_hi, xm_lo = sb("xm", [P, N]), sb("xm_hi", [P, N], F16), sb("xm_lo", [P, N], F16)
        xin, xin_hi, xin_lo = sb("xin", [P, J, N]), sb("xin_hi", [P, J, N], F16), sb("xin_lo", [P, J, N], F16)
        skip = sb("skip", [P, J, N])
        z = sb("z", [P, J, N])
        a = sb("a", [P, J, N])
        bb = sb("bb", [P, 2, N])
        hs = sb("hs", [P, 2, N])
        carry = sb("carry", [P, (CHUNKS // PER_SEQ) * (PER_SEQ + 1) * 2 * J])
        s32, s_hi, s_lo = sb("s32", [P, 2, N]), sb("s_hi", [P, J, N], F16), sb("s_lo", [P, J, N], F16)
        oT = sb("oT", [P, N])
        h2T = sb("h2T", [P, N])
        n3T, n3T_hi, n3T_lo = sb("n3T", [P, N]), sb("n3T_hi", [P, N], F16), sb("n3T_lo", [P, N], F16)
        xa, xa_hi, xa_lo = sb("xa", [P, N]), sb("xa_hi", [P, N], F16), sb("xa_lo", [P, N], F16)
        up, up_hi, up_lo = sb("up", [P, J, N]), sb("up_hi", [P, J, N], F16), sb("up_lo", [P, J, N], F16)
        y, y_hi, y_lo = sb("y", [P, N]), sb("y_hi", [P, N], F16), sb("y_lo", [P, N], F16)
        g = sb("g", [P, N])
        gated = sb("gated", [P, N])

        def weight(name, blocks, cols):
            return (sb(f"{name}_raw", [P, blocks, cols]), sb(f"{name}_hi", [P, blocks, cols], F16),
                    sb(f"{name}_lo", [P, blocks, cols], F16))

        w1, w2 = weight("w1", 1, EXP), weight("w2", 1, EXP)
        wz, wh = weight("wz", J, EXP), weight("wh", J, EXP)
        wo, wa, wn = weight("wo", J, D), weight("wa", 1, D), weight("wn", 1, D)
        eup, edn = weight("eup", 1, EXP), weight("edn", J, D)

        param_rows = sb("param_rows", [ROWS, P])
        col = sb("col", [P, ROWS])
        wmod_sb = sb("wmod_sb", [P, 6 * D])
        ident = sb("ident", [P, P])
        ones = sb("ones", [P, P])
        silu_c = sb("silu_c", [P, B])
        silu_c_wide = sb("silu_c_wide", [P, B, P])
        mod = sb("mod", [P, 6, B])
        magnitude, sign = sb("magnitude", [P, 6, B]), sb("sign", [P, 6, B])
        per_seq = sb("per_seq", [P, TABLES, B])
        table = sb("table", [P, TABLES * HALVES * CHUNKS])
        shift2_rows = sb("shift2_rows", [P, B, D])
        scale2_rows = sb("scale2_rows", [P, B, D])
        bh_scaled = sb("bh_scaled", [P, J])
        minus_bz = sb("minus_bz", [P, J])

        s_rows, s_wmod = sem("s_rows"), sem("s_wmod")
        s_x0_in, s_x1_in, s_xrest_in = sem("s_x0_in"), sem("s_x1_in"), sem("s_xrest_in")
        s_raw = {n: sem(f"s_raw_{n}") for n in ("w1", "w2", "wz", "wh", "wo", "wa", "wn")}
        s_eup_raw, s_edn_raw = sem("s_eup_raw"), sem("s_edn_raw")
        s_stored = sem("s_stored")
        s_ident0, s_ident, s_half = sem("s_ident0"), sem("s_ident"), sem("s_half")
        s_setup = sem("s_setup")
        s_cols_psum, s_silu_c, s_mod_psum = sem("s_cols_psum"), sem("s_silu_c"), sem("s_mod_psum")
        s_w_hi, s_w_lo = sem("s_w_hi"), sem("s_w_lo")
        s_stats = {n: sem(f"s_stats{n}") for n in (1, 2, 3)}
        s_mv = {n: sem(f"s_mv{n}") for n in (1, 2, 3)}
        s_var = {n: sem(f"s_var{n}") for n in (1, 2, 3)}
        s_rstd = {n: sem(f"s_rstd{n}") for n in (1, 2, 3)}
        s_n1, s_u2, s_h2, s_n3 = sem("s_n1"), sem("s_u2"), sem("s_h2"), sem("s_n3")
        s_passed = sem("s_passed")
        s_n1T_psum, s_xm, s_xm_lo = sem("s_n1T_psum"), sem("s_xm"), sem("s_xm_lo")
        s_xin_psum, s_xin, s_xin_hi, s_xin_lo = sem("s_xin_psum"), sem("s_xin"), sem("s_xin_hi"), sem("s_xin_lo")
        s_skip_psum, s_skip = sem("s_skip_psum"), sem("s_skip")
        s_z_psum, s_z = sem("s_z_psum"), sem("s_z")
        s_h_psum, s_b, s_scan, s_carry = sem("s_h_psum"), sem("s_b"), sem("s_scan"), sem("s_carry")
        s_sum, s_s_hi, s_s = sem("s_sum"), sem("s_s_hi"), sem("s_s")
        s_e_hi, s_e_lo = sem("s_e_hi"), sem("s_e_lo")
        s_o_psum, s_oT, s_oT_psum, s_x1 = sem("s_o_psum"), sem("s_oT"), sem("s_oT_psum"), sem("s_x1")
        s_h2T_psum, s_h2T, s_n3T_psum, s_n3T, s_n3T_lo = (
            sem("s_h2T_psum"), sem("s_h2T"), sem("s_n3T_psum"), sem("s_n3T"), sem("s_n3T_lo"))
        s_attn_psum, s_xa, s_xa_hi, s_xa_lo = sem("s_attn_psum"), sem("s_xa"), sem("s_xa_hi"), sem("s_xa_lo")
        s_up_psum, s_up, s_up_lo = sem("s_up_psum"), sem("s_up"), sem("s_up_lo")
        s_dn_psum, s_y, s_y_lo = sem("s_dn_psum"), sem("s_y"), sem("s_y_lo")
        s_next_psum, s_g, s_gated, s_out_psum, s_out = (
            sem("s_next_psum"), sem("s_g"), sem("s_gated"), sem("s_out_psum"), sem("s_out"))

        W_ORDER = [("w1", w1, 1), ("w2", w2, 1)] + [("wz", wz, J), ("wh", wh, J), ("wo", wo, 1), ("wa", wa, 1), ("wn", wn, 1)]
        W_COUNT, n = {}, 0
        for name, _, blocks in W_ORDER:
            W_COUNT[name] = n
            n += blocks

        ROW_LOADS = 12
        SETUP_WIDE = 2 + B
        SETUP_TABLES = SETUP_WIDE + 3 + 1 + 2 * B + 4 + TABLES + PER_SEQ

        def table_col(which, half, c):
            return table[:, bass.ds(which * HALVES * CHUNKS + half * CHUNKS + c, 1)]

        def row_tile(t, half, c):
            return t[:].rearrange("p b d -> p (b d)")[:, bass.ds((c // PER_SEQ + 2 * half) * D, D)]

        def x_tiles(c, i=0, count=TILES):
            return x_all[:].rearrange("p c t d -> p (c t d)")[:, bass.ds(c * (TILES * D) + i * D, count * D)]

        def carry_cols(c, j, half, count):
            return carry[:, bass.ds((c + c // PER_SEQ) * (2 * J) + 2 * j + half, count)]

        def weight_blocks(w, blocks):
            flat = [t[:].rearrange("p b n -> p (b n)") for t in w]
            width = flat[0].shape[1] // blocks
            return [[t[:, i * width:(i + 1) * width] for t in flat] for i in range(blocks)]

        def run_steps(eng, step):
            step(0, front=True, mid=False, last=False)
            step(1, front=True, mid=True, last=False)
            with eng.Fori(2, CHUNKS - 1) as k:
                step(k, front=True, mid=True, last=True)
            step(CHUNKS - 1, front=True, mid=True, last=True, norm_ahead=False)
            step(CHUNKS, front=False, mid=True, last=True)
            step(CHUNKS + 1, front=False, mid=False, last=True)

        block = ctx.enter_context(nc.Block())

        @block.sync
        def _(sp):
            def load_x(c, loaded):
                for half in range(HALVES):
                    tiles = slice(half * TILES // 2, (half + 1) * TILES // 2)
                    sp.dma_start(x_all[:, c, tiles], x_rows[half, c]).then_inc(loaded, 16)

            load_x(0, s_x0_in)
            for at, v in ((R_B1, b1), (R_B2, b2), (R_BZ, bz), (R_BH, bh), (R_BO, bo), (R_G, ln_g), (R_LB, ln_b),
                          (R_AB, attn_b), (R_NB, next_b)):
                count = v.shape[0] // P
                sp.dma_start(param_rows[at:at + count, :], rows(v)).then_inc(s_rows, 16)
            sp.dma_start(param_rows[R_EB2:R_EB2 + E, :], eb2).then_inc(s_rows, 16)
            sp.dma_start(param_rows[R_EB1:R_EB1 + E * J, :], eb1.rearrange("e (j n) -> (e j) n", n=P)).then_inc(s_rows, 16)
            sp.dma_start(param_rows[R_C:R_C + B, :], cond).then_inc(s_rows, 16)
            sp.dma_start(wmod_sb[:], wmod).then_inc(s_wmod, 16)
            sp.dma_start(w1[0][:, 0], W1).then_inc(s_raw["w1"], 16)
            sp.dma_start(w2[0][:, 0], W2).then_inc(s_raw["w2"], 16)
            sp.dma_start(wz[0][:], Wz.rearrange("(b p) n -> p b n", p=P)).then_inc(s_raw["wz"], 16)
            sp.dma_start(wh[0][:], Wh.rearrange("(b p) n -> p b n", p=P)).then_inc(s_raw["wh"], 16)
            load_x(1, s_x1_in)
            sp.dma_start(wo[0][:], Wo.rearrange("(b p) n -> p b n", p=P)).then_inc(s_raw["wo"], 16)
            sp.dma_start(wa[0][:, 0], attn_w).then_inc(s_raw["wa"], 16)
            sp.dma_start(wn[0][:, 0], next_w).then_inc(s_raw["wn"], 16)
            sp.dma_start(eup[0][:, 0], ew1[0]).then_inc(s_eup_raw, 16)
            sp.dma_start(edn[0][:], ew2[0].rearrange("(b p) n -> p b n", p=P)).then_inc(s_edn_raw, 16)
            for c in range(2, CHUNKS):
                load_x(c, s_xrest_in)

            def load_expert(e):
                sp.wait_ge(s_e_lo, 2 * e)
                sp.dma_start(eup[0][:, 0], ew1.rearrange("e p n -> (e p) n")[bass.ds(e * P, P), :]).then_inc(s_eup_raw, 16)
                sp.dma_start(edn[0][:], ew2.rearrange("e (b p) n -> e p b n", p=P)[e]).then_inc(s_edn_raw, 16)

            def store(u):
                sp.wait_ge(s_out, u + 1)
                for half in range(HALVES):
                    rows_out = x_tiles(u, half * TILES // 2, TILES // 2).rearrange("p (t d) -> p t d", d=D)
                    sp.dma_start(out_rows[half, u], rows_out).then_inc(s_stored, 16)

            load_expert(1)
            with sp.Fori(2, CHUNKS) as e:
                load_expert(e)
                store(e - 2)
            store(CHUNKS - 2)
            store(CHUNKS - 1)
            sp.wait_ge(s_stored, 16 * HALVES * CHUNKS)

        @block.gpsimd
        def _(pool):
            nc.gpsimd.memset(ident[:], 0.0).then_inc(s_ident0, 1)
            nc.gpsimd.memset(minus_half[:], -0.5).then_inc(s_half, 1)
            pool.wait_ge(s_ident0, 1)
            nc.gpsimd.affine_select(out=ident[:], in_=ident[:], compare_op=ALU.not_equal, fill=1.0, base=0,
                                    pattern=[[-1, P]], channel_multiplier=1).then_inc(s_ident, 1)

            def rsqrt(n, c):
                pool.wait_ge(s_var[n], c + 1)
                nc.gpsimd.tensor_tensor(rstd[n][:], var_eps[n][:], minus_half[:], ALU.pow).then_inc(s_rstd[n], 1)

            def step(k, front, mid, last, norm_ahead=True):
                t = k - 1
                if front:
                    for j in range(J):
                        pool.wait_ge(s_xin_hi, J * k + j + 1)
                        nc.gpsimd.tensor_tensor(xin_lo[:, j], xin[:, j], xin_hi[:, j], ALU.subtract).then_inc(s_xin_lo, 1)
                    if norm_ahead:
                        rsqrt(1, k + 1)
                if mid:
                    rsqrt(2, t)
                    rsqrt(3, t)
                    for j in range(J):
                        pool.wait_ge(s_up, 2 * (J * t + j + 1))
                        nc.gpsimd.tensor_tensor(up_lo[:, j], up[:, j], up_hi[:, j], ALU.subtract).then_inc(s_up_lo, 1)

            pool.wait_ge(s_half, 1)
            rsqrt(1, 0)
            run_steps(pool, step)

        @block.scalar
        def _(act):
            act.wait_ge(s_setup, 2)
            nc.scalar.activation(silu_c[:], col[:, R_C:R_C + B], ACT.Silu).then_inc(s_silu_c, 1)

            def split_hi(names):
                for name, w, blocks in W_ORDER:
                    if name in names:
                        act.wait_ge(s_raw[name], 16)
                        for raw, hi, _ in weight_blocks(w, blocks):
                            nc.scalar.activation(hi, raw, ACT.Copy, scale=WSCALE).then_inc(s_w_hi, 1)

            def modulate(c, first=False):
                act.wait_ge(s_n1T_psum, c + 1)
                if not first:
                    act.wait_ge(s_xm_lo, c)
                    act.wait_ge(s_skip_psum, J * c)
                for dst in (xm, xm_hi):
                    for half in range(HALVES):
                        cols = slice(half * SPAN, (half + 1) * SPAN)
                        nc.scalar.activation(dst[:, cols], bank_B[1][:, cols], ACT.Identity,
                                             scale=table_col(T_SCALE1, half, c),
                                             bias=table_col(T_SHIFT1, half, c)).then_inc(s_xm, 1)

            def step(k, front, mid, last, norm_ahead=True):
                t, u = k - 1, k - 2
                if front:
                    for j in range(J):
                        act.wait_ge(s_xin_psum, J * k + j + 1)
                        if mid:
                            act.wait_ge(s_xin_lo, J * (k - 1) + j + 1)
                        nc.scalar.activation(xin[:, j], bank_A[j % 2][:], ACT.Silu, scale=UNSCALE,
                                             bias=col[:, R_B1 + j:R_B1 + j + 1]).then_inc(s_xin, 1)
                    for j in range(J):
                        act.wait_ge(s_skip_psum, J * k + j + 1)
                        if mid:
                            act.wait_ge(s_sum, J * (k - 1) + j + 1)
                        nc.scalar.activation(skip[:, j], bank_A[j % 2][:], ACT.Silu, scale=UNSCALE,
                                             bias=col[:, R_B2 + j:R_B2 + j + 1]).then_inc(s_skip, 1)
                if mid:
                    act.wait_ge(s_o_psum, t + 1)
                    if last:
                        act.wait_ge(s_oT_psum, t)
                    for half in range(HALVES):
                        cols = slice(half * SPAN, (half + 1) * SPAN)
                        nc.scalar.activation(oT[:, cols], bank_D[:, cols], ACT.Identity,
                                             scale=table_col(T_GATE1, half, t),
                                             bias=table_col(T_GATE1_BO, half, t)).then_inc(s_oT, 1)
                if front:
                    for j in range(J):
                        act.wait_ge(s_z_psum, J * k + j + 1)
                        if mid:
                            act.wait_ge(s_scan, 2 * (J * (k - 1) + j + 1))
                        nc.scalar.activation(z[:, j], bank_B[j % 2][:], ACT.Sigmoid, scale=UNSCALE,
                                             bias=col[:, R_BZ + j:R_BZ + j + 1]).then_inc(s_z, 1)
                        nc.scalar.activation(a[:, j], bank_B[j % 2][:], ACT.Sigmoid, scale=-UNSCALE,
                                             bias=minus_bz[:, j:j + 1]).then_inc(s_z, 1)
                if mid:
                    act.wait_ge(s_h2T_psum, t + 1)
                    if last:
                        act.wait_ge(s_xa, t)
                    nc.scalar.activation(h2T[:], bank_E[:], ACT.Identity, bias=col[:, R_AB:R_AB + 1]).then_inc(s_h2T, 1)
                    act.wait_ge(s_n3T_psum, t + 1)
                    if last:
                        act.wait_ge(s_n3T_lo, t)
                        act.wait_ge(s_attn_psum, t)
                    for dst in (n3T, n3T_hi):
                        nc.scalar.activation(dst[:], bank_B[0][:], ACT.Identity, scale=col[:, R_G:R_G + 1],
                                             bias=col[:, R_LB:R_LB + 1]).then_inc(s_n3T, 1)
                if front and norm_ahead:
                    modulate(k + 1)
                if last:
                    act.wait_ge(s_next_psum, u + 1)
                    nc.scalar.activation(g[:], bank_D[:], ACT.Gelu, scale=UNSCALE,
                                         bias=col[:, R_NB:R_NB + 1]).then_inc(s_g, 1)
                if mid:
                    for j in range(J):
                        act.wait_ge(s_up_psum, J * t + j + 1)
                        if last:
                            act.wait_ge(s_up_lo, J * (t - 1) + j + 1)
                            act.wait_ge(s_dn_psum, t)
                        for dst in (up, up_hi):
                            nc.scalar.activation(dst[:, j], bank_A[j % 2][:], ACT.Gelu, scale=UNSCALE,
                                                 bias=col[:, bass.ds(R_EB1 + J * t + j, 1)]).then_inc(s_up, 1)
                    act.wait_ge(s_dn_psum, t + 1)
                    if last:
                        act.wait_ge(s_y_lo, t)
                    for dst in (y, y_hi):
                        nc.scalar.activation(dst[:], bank_D[:], ACT.Identity, scale=UNSCALE,
                                             bias=col[:, bass.ds(R_EB2 + t, 1)]).then_inc(s_y, 1)

            split_hi(("w1", "w2"))
            act.wait_ge(s_setup, SETUP_TABLES)
            modulate(0, first=True)
            split_hi(("wz", "wh", "wo", "wa", "wn"))
            run_steps(act, step)

        @block.vector
        def _(dve):
            setup = [0]

            def after_setup(ins):
                setup[0] += 1
                ins.then_inc(s_setup, 1)
                dve.wait_ge(s_setup, setup[0])

            def norm_stats(n, c, tile):
                for i in range(TILES):
                    nc.vector.bn_stats(stats[n][:, i], tile(i)).then_inc(s_stats[n], 1)
                dve.wait_ge(s_stats[n], TILES * (c + 1)).then_inc(s_passed, 1)
                for i in range(TILES):
                    nc.vector.bn_aggr(mean_var[n][:, i], stats[n][:, i]).then_inc(s_mv[n], 1)
                dve.wait_ge(s_mv[n], TILES * (c + 1))
                nc.vector.tensor_scalar(var_eps[n][:], mean_var[n][:, :, 1], EPS, None, ALU.add).then_inc(s_var[n], 1)

            def norm1(c, first=False):
                norm_stats(1, c, lambda i: x_tiles(c, i, 1))
                dve.wait_ge(s_rstd[1], c + 1)
                if not first:
                    dve.wait_ge(s_n1T_psum, c)
                for i in range(TILES):
                    nc.vector.tensor_scalar(n1[:, i], x_tiles(c, i, 1), mean_var[1][:, i, 0:1], rstd[1][:, i:i + 1],
                                            ALU.subtract, ALU.mult).then_inc(s_n1, 1)

            def modulated_low(c):
                dve.wait_ge(s_xm, 4 * (c + 1))
                nc.vector.tensor_tensor(xm_lo[:], xm[:], xm_hi[:], ALU.subtract).then_inc(s_xm_lo, 1)

            def split_lo(names):
                for name, w, blocks in W_ORDER:
                    if name in names:
                        for i, (raw, hi, lo) in enumerate(weight_blocks(w, blocks)):
                            dve.wait_ge(s_w_hi, W_COUNT[name] + i + 1)
                            nc.vector.scalar_tensor_tensor(out=lo, in0=raw, scalar=WSCALE, in1=hi, op0=ALU.mult,
                                                           op1=ALU.subtract).then_inc(s_w_lo, 1)

            def split_expert(t, first):
                if not first:
                    dve.wait_ge(s_dn_psum, t)
                for n, (w, loaded) in enumerate(((eup, s_eup_raw), (edn, s_edn_raw))):
                    raw, hi, lo = weight_blocks(w, 1)[0]
                    dve.wait_ge(loaded, 16 * (t + 1))
                    nc.vector.tensor_scalar(hi, raw, WSCALE, None, ALU.mult).then_inc(s_e_hi, 1)
                    dve.wait_ge(s_e_hi, 2 * t + n + 1)
                    nc.vector.scalar_tensor_tensor(out=lo, in0=raw, scalar=WSCALE, in1=hi, op0=ALU.mult,
                                                   op1=ALU.subtract).then_inc(s_e_lo, 1)

            def recur(k, j, mid):
                dve.wait_ge(s_h_psum, J * k + j + 1)
                dve.wait_ge(s_z, 2 * (J * k + j + 1))
                if mid or j >= 2:
                    dve.wait_ge(s_sum, J * k + j - 1)
                nc.vector.scalar_tensor_tensor(out=bb[:, j % 2], in0=bank_C[j % 2][:], scalar=bh_scaled[:, j:j + 1],
                                               in1=z[:, j], op0=ALU.add, op1=ALU.mult).then_inc(s_b, 1)
                dve.wait_ge(s_b, J * k + j + 1)
                if mid:
                    dve.wait_ge(s_carry, J * (k - 1) + j + 1)
                for half in range(HALVES):
                    cols = slice(half * SPAN, (half + 1) * SPAN)
                    nc.vector.tensor_tensor_scan(hs[:, j % 2, cols], a[:, j, cols], bb[:, j % 2, cols],
                                                 carry_cols(k, j, half, 1), ALU.mult, ALU.add).then_inc(s_scan, 1)
                dve.wait_ge(s_scan, 2 * (J * k + j + 1))
                slot = (k + k // PER_SEQ + 1) * (2 * J) + 2 * j
                nc.vector.tensor_copy(carry[:, bass.ds(slot, HALVES)],
                                      hs[:, j % 2].rearrange("p (h n) -> p h n", h=HALVES)[:, :, SPAN - 1]).then_inc(s_carry, 1)

            def mixed(k, j, mid):
                dve.wait_ge(s_skip, J * k + j + 1)
                if mid or j >= 2:
                    dve.wait_ge(s_s, J * k + j - 1)
                nc.vector.scalar_tensor_tensor(out=s32[:, j % 2], in0=hs[:, j % 2], scalar=UNSCALE, in1=skip[:, j],
                                               op0=ALU.mult, op1=ALU.add).then_inc(s_sum, 1)
                dve.wait_ge(s_sum, J * k + j + 1)
                if mid:
                    dve.wait_ge(s_o_psum, k)
                nc.vector.tensor_copy(s_hi[:, j], s32[:, j % 2]).then_inc(s_s_hi, 1)
                dve.wait_ge(s_s_hi, J * k + j + 1)
                nc.vector.tensor_tensor(s_lo[:, j], s32[:, j % 2], s_hi[:, j], ALU.subtract).then_inc(s_s, 1)

            def residual_and_norms(t):
                dve.wait_ge(s_oT_psum, t + 1)
                nc.vector.tensor_tensor(x_tiles(t), bank_E[:], x_tiles(t), ALU.add).then_inc(s_x1, 1)
                dve.wait_ge(s_x1, t + 1).then_inc(s_passed, 1)
                norm_stats(2, t, lambda i: x_tiles(t, i, 1))
                for i in range(TILES):
                    nc.vector.scalar_tensor_tensor(out=u2[:, i], in0=x_tiles(t, i, 1), scalar=mean_var[2][:, i, 0:1],
                                                   in1=row_tile(scale2_rows, i // 2, t), op0=ALU.subtract,
                                                   op1=ALU.mult).then_inc(s_u2, 1)
                dve.wait_ge(s_rstd[2], t + 1)
                for i in range(TILES):
                    dve.wait_ge(s_u2, TILES * t + i + 1)
                    nc.vector.scalar_tensor_tensor(out=h2[:, i], in0=u2[:, i], scalar=rstd[2][:, i:i + 1],
                                                   in1=row_tile(shift2_rows, i // 2, t), op0=ALU.mult,
                                                   op1=ALU.add).then_inc(s_h2, 1)
                dve.wait_ge(s_h2, TILES * (t + 1))
                norm_stats(3, t, lambda i: h2[:, i])
                dve.wait_ge(s_rstd[3], t + 1)
                for i in range(TILES):
                    nc.vector.tensor_scalar(n3[:, i], h2[:, i], mean_var[3][:, i, 0:1], rstd[3][:, i:i + 1],
                                            ALU.subtract, ALU.mult).then_inc(s_n3, 1)

            def attended(t):
                dve.wait_ge(s_attn_psum, t + 1)
                dve.wait_ge(s_h2T, t + 1)
                nc.vector.scalar_tensor_tensor(out=xa[:], in0=bank_D[:], scalar=UNSCALE, in1=h2T[:], op0=ALU.mult,
                                               op1=ALU.add).then_inc(s_xa, 1)
                dve.wait_ge(s_xa, t + 1)
                nc.vector.tensor_copy(xa_hi[:], xa[:]).then_inc(s_xa_hi, 1)
                dve.wait_ge(s_xa_hi, t + 1)
                nc.vector.tensor_tensor(xa_lo[:], xa[:], xa_hi[:], ALU.subtract).then_inc(s_xa_lo, 1)

            def step(k, front, mid, last, norm_ahead=True):
                t, u = k - 1, k - 2
                if front:
                    for j in range(J):
                        dve.wait_ge(s_xin, J * k + j + 1)
                        if mid:
                            dve.wait_ge(s_h_psum, J * k)
                        nc.vector.tensor_copy(xin_hi[:, j], xin[:, j]).then_inc(s_xin_hi, 1)
                if mid:
                    split_expert(t, first=not last)
                if last:
                    dve.wait_ge(s_y, 2 * (u + 1))
                    nc.vector.tensor_tensor(y_lo[:], y[:], y_hi[:], ALU.subtract).then_inc(s_y_lo, 1)
                if front and norm_ahead:
                    if not mid:
                        dve.wait_ge(s_x1_in, 16 * HALVES)
                        dve.wait_ge(s_xrest_in, 16 * HALVES * (CHUNKS - 2))
                    norm1(k + 1)
                if mid:
                    residual_and_norms(t)
                if front:
                    recur(k, 0, mid)
                if mid:
                    dve.wait_ge(s_n3T, 2 * (t + 1))
                    nc.vector.tensor_tensor(n3T_lo[:], n3T[:], n3T_hi[:], ALU.subtract).then_inc(s_n3T_lo, 1)
                if front:
                    mixed(k, 0, mid)
                    recur(k, 1, mid)
                if mid:
                    attended(t)
                if front:
                    if norm_ahead:
                        modulated_low(k + 1)
                    mixed(k, 1, mid)
                if last:
                    dve.wait_ge(s_g, u + 1)
                    for half in range(HALVES):
                        cols = slice(half * SPAN, (half + 1) * SPAN)
                        nc.vector.tensor_scalar(gated[:, cols], g[:, cols], table_col(T_GATE2, half, u), None,
                                                ALU.mult).then_inc(s_gated, 1)
                if front:
                    for j in (2, 3):
                        recur(k, j, mid)
                        mixed(k, j, mid)
                if last:
                    dve.wait_ge(s_out_psum, u + 1)
                    nc.vector.tensor_tensor(x_tiles(u), bank_E[:], x_tiles(u), ALU.add).then_inc(s_out, 1)

            after_setup(nc.vector.memset(ones[:], 1.0))
            dve.wait_ge(s_cols_psum, 1)
            after_setup(nc.vector.tensor_copy(col[:], bank_E[:, 0:ROWS]))
            dve.wait_ge(s_x0_in, 16 * HALVES)
            norm1(0, first=True)
            dve.wait_ge(s_silu_c, 1)
            for b in range(B):
                after_setup(nc.vector.tensor_scalar(silu_c_wide[:, b], ones[:], silu_c[:, b:b + 1], None, ALU.mult))
            assert setup[0] == SETUP_WIDE
            after_setup(nc.vector.memset(carry[:], 0.0))
            after_setup(nc.vector.tensor_scalar(bh_scaled[:], col[:, R_BH:R_BH + J], WSCALE, None, ALU.mult))
            after_setup(nc.vector.tensor_scalar(minus_bz[:], col[:, R_BZ:R_BZ + J], -1.0, None, ALU.mult))
            dve.wait_ge(s_mod_psum, 1)
            after_setup(nc.vector.tensor_copy(mod[:].rearrange("p m b -> p (m b)"), bank_D[:, 0:6 * B]))
            for b in range(B):
                both = bank_C[b // 2][:, (b % 2) * 2 * D:(b % 2 + 1) * 2 * D]
                after_setup(nc.vector.tensor_copy(shift2_rows[:, b], both[:, 0:D]))
                after_setup(nc.vector.tensor_scalar(scale2_rows[:, b], both[:, D:2 * D], 1.0, None, ALU.add))
            after_setup(nc.vector.scalar_tensor_tensor(out=magnitude[:], in0=mod[:], scalar=-1.0, in1=mod[:],
                                                       op0=ALU.mult, op1=ALU.max))
            after_setup(nc.vector.tensor_scalar(magnitude[:], magnitude[:], 0.25, None, ALU.max))
            after_setup(nc.vector.tensor_scalar(sign[:], mod[:], 0.0, 2.0, ALU.is_ge, ALU.mult))
            after_setup(nc.vector.scalar_tensor_tensor(out=sign[:], in0=sign[:], scalar=-1.0, in1=magnitude[:],
                                                       op0=ALU.add, op1=ALU.mult))
            after_setup(nc.vector.tensor_scalar(per_seq[:, T_SCALE1], mod[:, 1], 1.0, None, ALU.add))
            after_setup(nc.vector.tensor_copy(per_seq[:, T_SHIFT1], mod[:, 0]))
            after_setup(nc.vector.tensor_scalar(per_seq[:, T_GATE1], sign[:, 2], UNSCALE, None, ALU.mult))
            after_setup(nc.vector.tensor_scalar(per_seq[:, T_GATE1_BO], sign[:, 2], col[:, R_BO:R_BO + 1], None, ALU.mult))
            after_setup(nc.vector.tensor_copy(per_seq[:, T_GATE2], sign[:, 5]))
            for r in range(PER_SEQ):
                after_setup(nc.vector.tensor_copy(
                    table[:].rearrange("p (m r) -> p m r", r=PER_SEQ)[:, :, r],
                    per_seq[:].rearrange("p t b -> p (t b)")))
            assert setup[0] == SETUP_TABLES
            split_lo(("w1", "w2"))
            modulated_low(0)
            split_lo(("wz", "wh", "wo", "wa", "wn"))
            run_steps(dve, step)

        @block.tensor
        def _(pe):
            def product(psum, parts, w, w_cols, block=0, first=True, final=True):
                (v_hi, v_lo), (_, w_hi, w_lo) = parts, w
                nc.tensor.matmul(psum, w_hi[:, block, w_cols], v_hi, start=first, stop=False)
                nc.tensor.matmul(psum, w_hi[:, block, w_cols], v_lo, start=False, stop=False)
                return nc.tensor.matmul(psum, w_lo[:, block, w_cols], v_hi, start=False, stop=final)

            def plane(j):
                return slice(j * P, (j + 1) * P)

            def turn(psum, src):
                for i in range(TILES):
                    last = nc.tensor.transpose(psum[:, i * P:(i + 1) * P], src(i), ident[:])
                return last

            def transpose_n1(c, first=False):
                pe.wait_ge(s_n1, TILES * (c + 1))
                if not first:
                    pe.wait_ge(s_z, 2 * J * c)
                turn(bank_B[1], lambda i: n1[:, i]).then_inc(s_n1T_psum, 1)

            def gate_plane(k, j, mid, last):
                if j == 0 and last:
                    pe.wait_ge(s_n3T, 2 * (k - 1))
                elif j == 0 and mid:
                    pe.wait_ge(s_z, 2 * J * k)
                if j >= 2:
                    pe.wait_ge(s_z, 2 * (J * k + j - 1))
                for i in range(J):
                    if j == 0:
                        if not mid:
                            pe.wait_ge(s_w_lo, W_COUNT["wz"] + i + 1)
                        pe.wait_ge(s_xin_lo, J * k + i + 1)
                    mm = product(bank_B[j % 2][:], (xin_hi[:, i], xin_lo[:, i]), wz, plane(j), i, i == 0, i == J - 1)
                mm.then_inc(s_z_psum, 1)

            def hidden_plane(k, j, mid):
                if mid or j >= 2:
                    pe.wait_ge(s_b, J * k + j - 1)
                for i in range(J):
                    if j == 0 and not mid:
                        pe.wait_ge(s_w_lo, W_COUNT["wh"] + i + 1)
                    mm = product(bank_C[j % 2][:], (xin_hi[:, i], xin_lo[:, i]), wh, plane(j), i, i == 0, i == J - 1)
                mm.then_inc(s_h_psum, 1)

            def step(k, front, mid, last, norm_ahead=True):
                t, u = k - 1, k - 2
                if front:
                    pe.wait_ge(s_xm_lo, k + 1)
                    for j in range(J):
                        if not mid and j == 0:
                            pe.wait_ge(s_w_lo, W_COUNT["w1"] + 1)
                        if j < 2 and last:
                            pe.wait_ge(s_up, 2 * (J * (t - 1) + j + 3))
                        elif j < 2 and mid:
                            pe.wait_ge(s_skip, J * (k - 1) + j + 3)
                        if j >= 2:
                            pe.wait_ge(s_xin, J * k + j - 1)
                        product(bank_A[j % 2][:], (xm_hi[:], xm_lo[:]), w1, plane(j)).then_inc(s_xin_psum, 1)
                    for j in range(J):
                        if not mid and j == 0:
                            pe.wait_ge(s_w_lo, W_COUNT["w2"] + 1)
                        if j < 2:
                            pe.wait_ge(s_xin, J * k + j + 3)
                        else:
                            pe.wait_ge(s_skip, J * k + j - 1)
                        product(bank_A[j % 2][:], (xm_hi[:], xm_lo[:]), w2, plane(j)).then_inc(s_skip_psum, 1)
                if mid:
                    if not last:
                        pe.wait_ge(s_w_lo, W_COUNT["wn"] + 1)
                    else:
                        pe.wait_ge(s_y, 2 * t)
                    for i in range(J):
                        pe.wait_ge(s_s, J * t + i + 1)
                        mm = product(bank_D[:], (s_hi[:, i], s_lo[:, i]), wo, slice(0, D), i, i == 0, i == J - 1)
                    mm.then_inc(s_o_psum, 1)
                if front:
                    gate_plane(k, 0, mid, last)
                if mid:
                    pe.wait_ge(s_oT, 2 * (t + 1))
                    if not front:
                        pe.wait_ge(s_out, u)
                    turn(bank_E, lambda i: oT[:, i * P:(i + 1) * P]).then_inc(s_oT_psum, 1)
                if front:
                    for j in (1, 2, 3):
                        gate_plane(k, j, mid, last)
                    hidden_plane(k, 0, mid)
                if mid:
                    pe.wait_ge(s_h2, TILES * (t + 1))
                    turn(bank_E, lambda i: h2[:, i]).then_inc(s_h2T_psum, 1)
                    pe.wait_ge(s_n3, TILES * (t + 1))
                    pe.wait_ge(s_z, 2 * J * (t + 1) + (6 if front else 0))
                    turn(bank_B[0], lambda i: n3[:, i]).then_inc(s_n3T_psum, 1)
                if front:
                    hidden_plane(k, 1, mid)
                if mid:
                    pe.wait_ge(s_n3T_lo, t + 1)
                    product(bank_D[:], (n3T_hi[:], n3T_lo[:]), wa, slice(0, D)).then_inc(s_attn_psum, 1)
                if front and norm_ahead:
                    transpose_n1(k + 1)
                if front:
                    hidden_plane(k, 2, mid)
                if last:
                    pe.wait_ge(s_y_lo, u + 1)
                    if mid:
                        pe.wait_ge(s_xa, t + 1)
                    product(bank_D[:], (y_hi[:], y_lo[:]), wn, slice(0, D)).then_inc(s_next_psum, 1)
                if mid:
                    pe.wait_ge(s_xa_lo, t + 1)
                    pe.wait_ge(s_e_lo, 2 * (t + 1))
                    for j in range(J):
                        if j < 2 and front:
                            pe.wait_ge(s_skip, J * (t + 1) + j + 3)
                        elif j < 2:
                            pe.wait_ge(s_up, 2 * (J * (t - 1) + j + 3))
                        if j >= 2:
                            pe.wait_ge(s_up, 2 * (J * t + j - 1))
                        product(bank_A[j % 2][:], (xa_hi[:], xa_lo[:]), eup, plane(j)).then_inc(s_up_psum, 1)
                if front:
                    hidden_plane(k, 3, mid)
                if last:
                    pe.wait_ge(s_gated, 2 * (u + 1))
                    if mid:
                        pe.wait_ge(s_h2T, t + 1)
                    else:
                        pe.wait_ge(s_out, u)
                    turn(bank_E, lambda i: gated[:, i * P:(i + 1) * P]).then_inc(s_out_psum, 1)
                if mid:
                    if last:
                        pe.wait_ge(s_g, u + 1)
                    for i in range(J):
                        pe.wait_ge(s_up_lo, J * t + i + 1)
                        mm = product(bank_D[:], (up_hi[:, i], up_lo[:, i]), edn, slice(0, D), i, i == 0, i == J - 1)
                    mm.then_inc(s_dn_psum, 1)

            pe.wait_ge(s_ident, 1)
            pe.wait_ge(s_rows, 16 * ROW_LOADS)
            nc.tensor.transpose(bank_E[:, 0:ROWS], param_rows[:], ident[0:ROWS, 0:ROWS]).then_inc(s_cols_psum, 1)
            transpose_n1(0, first=True)
            pe.wait_ge(s_wmod, 16)
            pe.wait_ge(s_setup, SETUP_WIDE)
            for m in range(6):
                nc.tensor.matmul(bank_D[:, m * B:(m + 1) * B], wmod_sb[:, m * D:(m + 1) * D], silu_c[:], start=True, stop=True)
            for b in range(B):
                mm = nc.tensor.matmul(bank_C[b // 2][:, (b % 2) * 2 * D:(b % 2 + 1) * 2 * D], silu_c_wide[:, b],
                                      wmod_sb[:, 3 * D:5 * D], start=True, stop=True)
            mm.then_inc(s_mod_psum, 1)
            run_steps(pe, step)


_INS = ["L0_attn_x", "L0_attn_W1", "L0_attn_b1", "L0_attn_W2", "L0_attn_b2", "L0_attn_Wz", "L0_attn_bz", "L0_attn_Wh",
        "L0_attn_bh", "L0_attn_Wo", "L0_attn_bo", "L0_ffn_ln_g", "L0_ffn_ln_b", "L0_ffn_attn_w", "L0_ffn_attn_b",
        "L0_ffn_w1", "L0_ffn_b1", "L0_ffn_w2", "L0_ffn_b2", "L0_ffn_next_w", "L0_ffn_next_b", "L0_c", "L0_wmod"]
_OUTS = [((4, 1024, 128), "float32")]


def kernel(**inputs):
    import numpy as _np
    import concourse.bacc as _bacc
    from concourse import mybir as _mybir
    from concourse.bass_utils import run_bass_kernel_spmd as _run

    nc = _bacc.Bacc("TRN2", target_bir_lowering=False, num_devices=1)
    arrays, args = {}, []
    for name in _INS:
        a = _np.ascontiguousarray(inputs[name])
        arrays[f"in_{name}_dram"] = a
        args.append(nc.dram_tensor(f"in_{name}_dram", a.shape, _mybir.dt.from_np(a.dtype), kind="ExternalInput").ap())
    for i, (shape, dtype) in enumerate(_OUTS):
        dt = _mybir.dt.from_np(_np.dtype(dtype))
        args.append(nc.dram_tensor(f"out_{i}_dram", shape, dt, kind="ExternalOutput").ap())
    adaln_mingru_experts(nc, *args)
    r = _run(nc, [arrays], core_ids=[0])
    got = tuple(r.results[0][f"out_{i}_dram"] for i in range(len(_OUTS)))
    return got[0]
```

```python
from contextlib import ExitStack

import concourse.bass as bass
from concourse import mybir

F32 = mybir.dt.float32
F16 = mybir.dt.float16
ALU = mybir.AluOpType
ACT = mybir.ActivationFunctionType

P = 128
WSCALE = 64.0
UNSCALE = 1.0 / WSCALE
EPS = 1e-5


def adaln_mingru_experts(nc, x, W1, b1, W2, b2, Wz, bz, Wh, bh, Wo, bo, ln_g, ln_b, attn_w, attn_b,
                         ew1, eb1, ew2, eb2, next_w, next_b, cond, wmod, out):
    B, S, D = x.shape
    EXP = W1.shape[1]
    E = ew1.shape[0]
    J = EXP // P
    HALVES = 2
    CHUNKS = E
    SPAN = B * S // (HALVES * CHUNKS)
    TILES = HALVES * SPAN // P
    N = HALVES * SPAN
    PER_SEQ = S // SPAN
    assert D == P and N == 512 and ew1.shape[2] == EXP and CHUNKS % PER_SEQ == 0 and B == 4

    R_B1, R_B2, R_BZ, R_BH = 0, J, 2 * J, 3 * J
    R_BO = 4 * J
    R_G, R_LB, R_AB, R_NB = R_BO + 1, R_BO + 2, R_BO + 3, R_BO + 4
    R_EB2 = R_BO + 5
    R_EB1 = R_EB2 + E
    ROWS = R_EB1 + E * J
    T_SCALE1, T_SHIFT1, T_GATE1, T_GATE1_BO, T_GATE2 = range(5)
    TABLES = 5

    def rows(v):
        return v.rearrange("(a n) -> a n", n=P)

    def token_rows(t):
        return t.rearrange("b s d -> (b s) d").rearrange("(h k t p) d -> h k p t d", h=HALVES, k=CHUNKS, p=P)

    x_rows, out_rows = token_rows(x), token_rows(out)

    with ExitStack() as ctx:
        def sb(name, shape, dt=F32):
            return ctx.enter_context(nc.sbuf_tensor(name, shape, dt))

        def sem(name):
            return ctx.enter_context(nc.semaphore(name))

        def bank(name):
            return ctx.enter_context(nc.psum_tensor(name, [P, N], F32))

        bank_A = [bank("bank_A0"), bank("bank_A1")]
        bank_B = [bank("bank_B0"), bank("bank_B1")]
        bank_AB = bank_A + bank_B
        bank_C = [bank("bank_C0"), bank("bank_C1")]
        bank_D = bank("bank_D")
        bank_E = bank("bank_E")

        x_all = sb("x_all", [P, CHUNKS, TILES, D])
        n1 = sb("n1", [P, TILES, D])
        u2 = sb("u2", [P, TILES, D])
        h2 = sb("h2", [P, TILES, D])
        n3 = sb("n3", [P, TILES, D])
        stats = {n: sb(f"stats{n}", [P, TILES, 6]) for n in (1, 2, 3)}
        mean_var = {n: sb(f"mean_var{n}", [P, TILES, 2]) for n in (1, 2, 3)}
        var_eps = {n: sb(f"var_eps{n}", [P, TILES]) for n in (1, 2, 3)}
        rstd = {n: sb(f"rstd{n}", [P, TILES]) for n in (1, 2, 3)}
        minus_half = sb("minus_half", [P, TILES])

        xm, xm_hi, xm_lo = sb("xm", [P, N]), sb("xm_hi", [P, N], F16), sb("xm_lo", [P, N], F16)
        xin, xin_hi, xin_lo = sb("xin", [P, J, N]), sb("xin_hi", [P, J, N], F16), sb("xin_lo", [P, J, N], F16)
        skip = sb("skip", [P, J, N])
        z = sb("z", [P, J, N])
        a = sb("a", [P, J, N])
        bb = sb("bb", [P, 2, N])
        hs = sb("hs", [P, 2, N])
        carry = sb("carry", [P, (CHUNKS // PER_SEQ) * (PER_SEQ + 1) * 2 * J])
        s32, s_hi, s_lo = sb("s32", [P, 2, N]), sb("s_hi", [P, J, N], F16), sb("s_lo", [P, J, N], F16)
        oT = sb("oT", [P, N])
        h2T = sb("h2T", [P, N])
        n3T, n3T_hi, n3T_lo = sb("n3T", [P, N]), sb("n3T_hi", [P, N], F16), sb("n3T_lo", [P, N], F16)
        xa, xa_hi, xa_lo = sb("xa", [P, N]), sb("xa_hi", [P, N], F16), sb("xa_lo", [P, N], F16)
        up, up_hi, up_lo = sb("up", [P, J, N]), sb("up_hi", [P, J, N], F16), sb("up_lo", [P, J, N], F16)
        y, y_hi, y_lo = sb("y", [P, N]), sb("y_hi", [P, N], F16), sb("y_lo", [P, N], F16)
        g = sb("g", [P, N])
        gated = sb("gated", [P, N])

        def weight(name, blocks, cols):
            return (sb(f"{name}_raw", [P, blocks, cols]), sb(f"{name}_hi", [P, blocks, cols], F16),
                    sb(f"{name}_lo", [P, blocks, cols], F16))

        w1, w2 = weight("w1", 1, EXP), weight("w2", 1, EXP)
        wz, wh = weight("wz", J, EXP), weight("wh", J, EXP)
        wo, wa, wn = weight("wo", J, D), weight("wa", 1, D), weight("wn", 1, D)
        eup, edn = weight("eup", 1, EXP), weight("edn", J, D)

        cond_rows = sb("cond_rows", [B, P])
        param_rows = sb("param_rows", [ROWS, P])
        col = sb("col", [P, ROWS])
        wmod_sb = sb("wmod_sb", [P, 6 * D])
        ident = sb("ident", [P, P])
        ones = sb("ones", [P, P])
        silu_c = sb("silu_c", [P, B])
        silu_c_wide = sb("silu_c_wide", [P, B, P])
        mod = sb("mod", [P, 6, B])
        magnitude, sign = sb("magnitude", [P, 6, B]), sb("sign", [P, 6, B])
        per_seq = sb("per_seq", [P, TABLES, B])
        table = sb("table", [P, TABLES * HALVES * CHUNKS])
        shift2_rows = sb("shift2_rows", [P, B, D])
        scale2_rows = sb("scale2_rows", [P, B, D])
        bh_scaled = sb("bh_scaled", [P, J])
        minus_bz = sb("minus_bz", [P, J])

        s_cond, s_rows, s_wmod = sem("s_cond"), sem("s_rows"), sem("s_wmod")
        s_x0_in, s_x1_in, s_xrest_in = sem("s_x0_in"), sem("s_x1_in"), sem("s_xrest_in")
        s_raw = {n: sem(f"s_raw_{n}") for n in ("w1", "w2", "wz", "wh", "wo", "wa", "wn")}
        s_eup_raw, s_edn_raw = sem("s_eup_raw"), sem("s_edn_raw")
        s_stored = sem("s_stored")
        s_ident0, s_ident, s_half = sem("s_ident0"), sem("s_ident"), sem("s_half")
        s_setup = sem("s_setup")
        s_cond_psum, s_silu_c, s_mod_psum = sem("s_cond_psum"), sem("s_silu_c"), sem("s_mod_psum")
        s_cols_psum, s_mod_rows_psum = sem("s_cols_psum"), sem("s_mod_rows_psum")
        s_wide, s_table1, s_cols, s_tables = sem("s_wide"), sem("s_table1"), sem("s_cols"), sem("s_tables")
        s_wz_hi, s_rows_ready = sem("s_wz_hi"), sem("s_rows_ready")
        s_w_hi, s_w_lo = sem("s_w_hi"), sem("s_w_lo")
        s_stats = {n: sem(f"s_stats{n}") for n in (1, 2, 3)}
        s_mv = {n: sem(f"s_mv{n}") for n in (1, 2, 3)}
        s_var = {n: sem(f"s_var{n}") for n in (1, 2, 3)}
        s_rstd = {n: sem(f"s_rstd{n}") for n in (1, 2, 3)}
        s_n1, s_u2, s_h2, s_n3 = sem("s_n1"), sem("s_u2"), sem("s_h2"), sem("s_n3")
        s_passed = sem("s_passed")
        s_n1T_psum, s_xm, s_xm_lo = sem("s_n1T_psum"), sem("s_xm"), sem("s_xm_lo")
        s_xin_psum, s_xin, s_xin_hi, s_xin_lo = sem("s_xin_psum"), sem("s_xin"), sem("s_xin_hi"), sem("s_xin_lo")
        s_skip_psum, s_skip = sem("s_skip_psum"), sem("s_skip")
        s_z_psum, s_z = sem("s_z_psum"), sem("s_z")
        s_h_psum, s_b, s_scan, s_carry = sem("s_h_psum"), sem("s_b"), sem("s_scan"), sem("s_carry")
        s_sum, s_s_hi, s_s = sem("s_sum"), sem("s_s_hi"), sem("s_s")
        s_e_hi, s_e_lo = sem("s_e_hi"), sem("s_e_lo")
        s_o_psum, s_oT, s_oT_psum, s_x1 = sem("s_o_psum"), sem("s_oT"), sem("s_oT_psum"), sem("s_x1")
        s_h2T_psum, s_h2T, s_n3T_psum, s_n3T, s_n3T_lo = (
            sem("s_h2T_psum"), sem("s_h2T"), sem("s_n3T_psum"), sem("s_n3T"), sem("s_n3T_lo"))
        s_attn_psum, s_xa, s_xa_hi, s_xa_lo = sem("s_attn_psum"), sem("s_xa"), sem("s_xa_hi"), sem("s_xa_lo")
        s_up_psum, s_up, s_up_lo = sem("s_up_psum"), sem("s_up"), sem("s_up_lo")
        s_dn_psum, s_y, s_y_lo = sem("s_dn_psum"), sem("s_y"), sem("s_y_lo")
        s_next_psum, s_g, s_gated, s_out_psum, s_out = (
            sem("s_next_psum"), sem("s_g"), sem("s_gated"), sem("s_out_psum"), sem("s_out"))

        W_ORDER = [("w1", w1, 1), ("w2", w2, 1)] + [("wz", wz, J), ("wh", wh, J), ("wo", wo, 1), ("wa", wa, 1), ("wn", wn, 1)]
        LO_BEFORE, HI_BEFORE, n, m = {}, {}, 0, 0
        for name, _, blocks in W_ORDER:
            LO_BEFORE[name], HI_BEFORE[name] = n, m
            n += blocks
            m += 0 if name == "wz" else blocks

        ROW_LOADS = 11

        def table_col(which, half, c):
            return table[:, bass.ds(which * HALVES * CHUNKS + half * CHUNKS + c, 1)]

        def row_tile(t, half, c):
            return t[:].rearrange("p b d -> p (b d)")[:, bass.ds((c // PER_SEQ + 2 * half) * D, D)]

        def x_tiles(c, i=0, count=TILES):
            return x_all[:].rearrange("p c t d -> p (c t d)")[:, bass.ds(c * (TILES * D) + i * D, count * D)]

        def carry_cols(c, j, half, count):
            return carry[:, bass.ds((c + c // PER_SEQ) * (2 * J) + 2 * j + half, count)]

        def weight_blocks(w, blocks):
            flat = [t[:].rearrange("p b n -> p (b n)") for t in w]
            width = flat[0].shape[1] // blocks
            return [[t[:, i * width:(i + 1) * width] for t in flat] for i in range(blocks)]

        def run_steps(eng, step):
            step(0, front=True, mid=False, last=False)
            step(1, front=True, mid=True, last=False)
            with eng.Fori(2, CHUNKS - 1) as k:
                step(k, front=True, mid=True, last=True)
            step(CHUNKS - 1, front=True, mid=True, last=True, norm_ahead=False)
            step(CHUNKS, front=False, mid=True, last=True)
            step(CHUNKS + 1, front=False, mid=False, last=True)

        block = ctx.enter_context(nc.Block())

        @block.sync
        def _(sp):
            def load_x(c, loaded):
                for half in range(HALVES):
                    tiles = slice(half * TILES // 2, (half + 1) * TILES // 2)
                    sp.dma_start(x_all[:, c, tiles], x_rows[half, c]).then_inc(loaded, 16)

            sp.dma_start(cond_rows[:], cond).then_inc(s_cond, 16)
            load_x(0, s_x0_in)
            sp.dma_start(wmod_sb[:], wmod).then_inc(s_wmod, 16)
            sp.dma_start(w1[0][:, 0], W1).then_inc(s_raw["w1"], 16)
            for at, v in ((R_B1, b1), (R_B2, b2), (R_BZ, bz), (R_BH, bh), (R_BO, bo), (R_G, ln_g), (R_LB, ln_b),
                          (R_AB, attn_b), (R_NB, next_b)):
                count = v.shape[0] // P
                sp.dma_start(param_rows[at:at + count, :], rows(v)).then_inc(s_rows, 16)
            sp.dma_start(param_rows[R_EB2:R_EB2 + E, :], eb2).then_inc(s_rows, 16)
            sp.dma_start(param_rows[R_EB1:R_EB1 + E * J, :], eb1.rearrange("e (j n) -> (e j) n", n=P)).then_inc(s_rows, 16)
            sp.dma_start(w2[0][:, 0], W2).then_inc(s_raw["w2"], 16)
            sp.dma_start(wz[0][:], Wz.rearrange("(b p) n -> p b n", p=P)).then_inc(s_raw["wz"], 16)
            sp.dma_start(wh[0][:], Wh.rearrange("(b p) n -> p b n", p=P)).then_inc(s_raw["wh"], 16)
            load_x(1, s_x1_in)
            sp.dma_start(wo[0][:], Wo.rearrange("(b p) n -> p b n", p=P)).then_inc(s_raw["wo"], 16)
            sp.dma_start(wa[0][:, 0], attn_w).then_inc(s_raw["wa"], 16)
            sp.dma_start(wn[0][:, 0], next_w).then_inc(s_raw["wn"], 16)
            sp.dma_start(eup[0][:, 0], ew1[0]).then_inc(s_eup_raw, 16)
            sp.dma_start(edn[0][:], ew2[0].rearrange("(b p) n -> p b n", p=P)).then_inc(s_edn_raw, 16)
            for c in range(2, CHUNKS):
                load_x(c, s_xrest_in)

            def load_expert(e):
                sp.wait_ge(s_e_lo, 2 * e)
                sp.dma_start(eup[0][:, 0], ew1.rearrange("e p n -> (e p) n")[bass.ds(e * P, P), :]).then_inc(s_eup_raw, 16)
                sp.dma_start(edn[0][:], ew2.rearrange("e (b p) n -> e p b n", p=P)[e]).then_inc(s_edn_raw, 16)

            def store(u):
                sp.wait_ge(s_out, u + 1)
                for half in range(HALVES):
                    rows_out = x_tiles(u, half * TILES // 2, TILES // 2).rearrange("p (t d) -> p t d", d=D)
                    sp.dma_start(out_rows[half, u], rows_out).then_inc(s_stored, 16)

            load_expert(1)
            with sp.Fori(2, CHUNKS) as e:
                load_expert(e)
                store(e - 2)
            store(CHUNKS - 2)
            store(CHUNKS - 1)
            sp.wait_ge(s_stored, 16 * HALVES * CHUNKS)

        @block.gpsimd
        def _(pool):
            nc.gpsimd.memset(ident[:], 0.0).then_inc(s_ident0, 1)
            nc.gpsimd.memset(minus_half[:], -0.5).then_inc(s_half, 1)
            pool.wait_ge(s_ident0, 1)
            nc.gpsimd.affine_select(out=ident[:], in_=ident[:], compare_op=ALU.not_equal, fill=1.0, base=0,
                                    pattern=[[-1, P]], channel_multiplier=1).then_inc(s_ident, 1)

            def rsqrt(n, c):
                pool.wait_ge(s_var[n], c + 1)
                nc.gpsimd.tensor_tensor(rstd[n][:], var_eps[n][:], minus_half[:], ALU.pow).then_inc(s_rstd[n], 1)

            def step(k, front, mid, last, norm_ahead=True):
                t = k - 1
                if front:
                    for j in range(J):
                        pool.wait_ge(s_xin_hi, J * k + j + 1)
                        nc.gpsimd.tensor_tensor(xin_lo[:, j], xin[:, j], xin_hi[:, j], ALU.subtract).then_inc(s_xin_lo, 1)
                    if norm_ahead:
                        rsqrt(1, k + 1)
                if mid:
                    rsqrt(2, t)
                    rsqrt(3, t)
                    for j in range(J):
                        pool.wait_ge(s_up, 2 * (J * t + j + 1))
                        nc.gpsimd.tensor_tensor(up_lo[:, j], up[:, j], up_hi[:, j], ALU.subtract).then_inc(s_up_lo, 1)

            pool.wait_ge(s_half, 1)
            rsqrt(1, 0)
            pool.wait_ge(s_raw["wz"], 16)
            for raw, hi, _ in weight_blocks(wz, J):
                nc.gpsimd.tensor_scalar(hi, raw, WSCALE, 1.0, ALU.mult, ALU.mult).then_inc(s_wz_hi, 1)
            run_steps(pool, step)

        @block.scalar
        def _(act):
            act.wait_ge(s_cond_psum, 1)
            nc.scalar.activation(silu_c[:], bank_E[:, 0:B], ACT.Silu).then_inc(s_silu_c, 1)

            def split_hi(names):
                for name, w, blocks in W_ORDER:
                    if name in names:
                        act.wait_ge(s_raw[name], 16)
                        for raw, hi, _ in weight_blocks(w, blocks):
                            nc.scalar.activation(hi, raw, ACT.Copy, scale=WSCALE).then_inc(s_w_hi, 1)

            def modulate(c, first=False):
                act.wait_ge(s_n1T_psum, c + 1)
                if not first:
                    act.wait_ge(s_xm_lo, c)
                    act.wait_ge(s_skip_psum, J * c)
                for dst in (xm, xm_hi):
                    for half in range(HALVES):
                        cols = slice(half * SPAN, (half + 1) * SPAN)
                        nc.scalar.activation(dst[:, cols], bank_B[1][:, cols], ACT.Identity,
                                             scale=table_col(T_SCALE1, half, c),
                                             bias=table_col(T_SHIFT1, half, c)).then_inc(s_xm, 1)

            def step(k, front, mid, last, norm_ahead=True):
                t, u = k - 1, k - 2
                if front:
                    for j in range(J):
                        act.wait_ge(s_xin_psum, J * k + j + 1)
                        if mid:
                            act.wait_ge(s_xin_lo, J * (k - 1) + j + 1)
                        nc.scalar.activation(xin[:, j], bank_AB[j][:], ACT.Silu, scale=UNSCALE,
                                             bias=col[:, R_B1 + j:R_B1 + j + 1]).then_inc(s_xin, 1)
                if last:
                    act.wait_ge(s_dn_psum, u + 1)
                    for dst in (y, y_hi):
                        nc.scalar.activation(dst[:], bank_D[:], ACT.Identity, scale=UNSCALE,
                                             bias=col[:, bass.ds(R_EB2 + u, 1)]).then_inc(s_y, 1)
                if front:
                    for j in range(J):
                        act.wait_ge(s_skip_psum, J * k + j + 1)
                        if mid:
                            act.wait_ge(s_sum, J * (k - 1) + j + 1)
                        nc.scalar.activation(skip[:, j], bank_AB[j][:], ACT.Silu, scale=UNSCALE,
                                             bias=col[:, R_B2 + j:R_B2 + j + 1]).then_inc(s_skip, 1)
                    if not mid:
                        split_hi(("wh",))
                if mid:
                    if not last:
                        act.wait_ge(s_tables, PER_SEQ)
                    act.wait_ge(s_o_psum, t + 1)
                    if last:
                        act.wait_ge(s_oT_psum, t)
                    for half in range(HALVES):
                        cols = slice(half * SPAN, (half + 1) * SPAN)
                        nc.scalar.activation(oT[:, cols], bank_D[:, cols], ACT.Identity,
                                             scale=table_col(T_GATE1, half, t),
                                             bias=table_col(T_GATE1_BO, half, t)).then_inc(s_oT, 1)
                if front:
                    for j in range(J):
                        act.wait_ge(s_z_psum, J * k + j + 1)
                        if mid:
                            act.wait_ge(s_scan, 2 * (J * (k - 1) + j + 1))
                        nc.scalar.activation(z[:, j], bank_B[j % 2][:], ACT.Sigmoid, scale=UNSCALE,
                                             bias=col[:, R_BZ + j:R_BZ + j + 1]).then_inc(s_z, 1)
                        nc.scalar.activation(a[:, j], bank_B[j % 2][:], ACT.Sigmoid, scale=-UNSCALE,
                                             bias=minus_bz[:, j:j + 1]).then_inc(s_z, 1)
                    if not mid:
                        split_hi(("wo", "wa", "wn"))
                if mid:
                    act.wait_ge(s_h2T_psum, t + 1)
                    if last:
                        act.wait_ge(s_xa, t)
                    nc.scalar.activation(h2T[:], bank_E[:], ACT.Identity, bias=col[:, R_AB:R_AB + 1]).then_inc(s_h2T, 1)
                    act.wait_ge(s_n3T_psum, t + 1)
                    if last:
                        act.wait_ge(s_n3T_lo, t)
                        act.wait_ge(s_attn_psum, t)
                    for dst in (n3T, n3T_hi):
                        nc.scalar.activation(dst[:], bank_B[0][:], ACT.Identity, scale=col[:, R_G:R_G + 1],
                                             bias=col[:, R_LB:R_LB + 1]).then_inc(s_n3T, 1)
                if front and norm_ahead:
                    modulate(k + 1)
                if last:
                    act.wait_ge(s_next_psum, u + 1)
                    nc.scalar.activation(g[:], bank_D[:], ACT.Gelu, scale=UNSCALE,
                                         bias=col[:, R_NB:R_NB + 1]).then_inc(s_g, 1)
                if mid:
                    for j in range(J):
                        act.wait_ge(s_up_psum, J * t + j + 1)
                        if last:
                            act.wait_ge(s_up_lo, J * (t - 1) + j + 1)
                            act.wait_ge(s_dn_psum, t)
                        for dst in (up, up_hi):
                            nc.scalar.activation(dst[:, j], bank_AB[j][:], ACT.Gelu, scale=UNSCALE,
                                                 bias=col[:, bass.ds(R_EB1 + J * t + j, 1)]).then_inc(s_up, 1)

            split_hi(("w1",))
            act.wait_ge(s_table1, PER_SEQ)
            modulate(0, first=True)
            split_hi(("w2",))
            act.wait_ge(s_cols, 3)
            run_steps(act, step)

        @block.vector
        def _(dve):
            setup = [0]

            def after_setup(ins):
                setup[0] += 1
                ins.then_inc(s_setup, 1)
                dve.wait_ge(s_setup, setup[0])

            def norm_stats(n, c, tile):
                for i in range(TILES):
                    nc.vector.bn_stats(stats[n][:, i], tile(i)).then_inc(s_stats[n], 1)
                dve.wait_ge(s_stats[n], TILES * (c + 1)).then_inc(s_passed, 1)
                for i in range(TILES):
                    nc.vector.bn_aggr(mean_var[n][:, i], stats[n][:, i]).then_inc(s_mv[n], 1)
                dve.wait_ge(s_mv[n], TILES * (c + 1))
                nc.vector.tensor_scalar(var_eps[n][:], mean_var[n][:, :, 1], EPS, None, ALU.add).then_inc(s_var[n], 1)

            def norm1(c, first=False):
                norm_stats(1, c, lambda i: x_tiles(c, i, 1))
                if first:
                    dve.wait_ge(s_silu_c, 1)
                    for b in range(B):
                        nc.vector.tensor_scalar(silu_c_wide[:, b], ones[:], silu_c[:, b:b + 1], None,
                                                ALU.mult).then_inc(s_wide, 1)
                dve.wait_ge(s_rstd[1], c + 1)
                if not first:
                    dve.wait_ge(s_n1T_psum, c)
                for i in range(TILES):
                    nc.vector.tensor_scalar(n1[:, i], x_tiles(c, i, 1), mean_var[1][:, i, 0:1], rstd[1][:, i:i + 1],
                                            ALU.subtract, ALU.mult).then_inc(s_n1, 1)

            def modulated_low(c):
                dve.wait_ge(s_xm, 4 * (c + 1))
                nc.vector.tensor_tensor(xm_lo[:], xm[:], xm_hi[:], ALU.subtract).then_inc(s_xm_lo, 1)

            def split_lo(names):
                for name, w, blocks in W_ORDER:
                    if name in names:
                        for i, (raw, hi, lo) in enumerate(weight_blocks(w, blocks)):
                            if name == "wz":
                                dve.wait_ge(s_wz_hi, i + 1)
                            else:
                                dve.wait_ge(s_w_hi, HI_BEFORE[name] + i + 1)
                            nc.vector.scalar_tensor_tensor(out=lo, in0=raw, scalar=WSCALE, in1=hi, op0=ALU.mult,
                                                           op1=ALU.subtract).then_inc(s_w_lo, 1)

            def split_expert(t, first):
                if not first:
                    dve.wait_ge(s_dn_psum, t)
                for n, (w, loaded) in enumerate(((eup, s_eup_raw), (edn, s_edn_raw))):
                    raw, hi, lo = weight_blocks(w, 1)[0]
                    dve.wait_ge(loaded, 16 * (t + 1))
                    nc.vector.tensor_scalar(hi, raw, WSCALE, None, ALU.mult).then_inc(s_e_hi, 1)
                    dve.wait_ge(s_e_hi, 2 * t + n + 1)
                    nc.vector.scalar_tensor_tensor(out=lo, in0=raw, scalar=WSCALE, in1=hi, op0=ALU.mult,
                                                   op1=ALU.subtract).then_inc(s_e_lo, 1)

            def recur(k, j, mid):
                dve.wait_ge(s_h_psum, J * k + j + 1)
                dve.wait_ge(s_z, 2 * (J * k + j + 1))
                if mid or j >= 2:
                    dve.wait_ge(s_sum, J * k + j - 1)
                nc.vector.scalar_tensor_tensor(out=bb[:, j % 2], in0=bank_C[j % 2][:], scalar=bh_scaled[:, j:j + 1],
                                               in1=z[:, j], op0=ALU.add, op1=ALU.mult).then_inc(s_b, 1)
                dve.wait_ge(s_b, J * k + j + 1)
                if mid:
                    dve.wait_ge(s_carry, J * (k - 1) + j + 1)
                for half in range(HALVES):
                    cols = slice(half * SPAN, (half + 1) * SPAN)
                    nc.vector.tensor_tensor_scan(hs[:, j % 2, cols], a[:, j, cols], bb[:, j % 2, cols],
                                                 carry_cols(k, j, half, 1), ALU.mult, ALU.add).then_inc(s_scan, 1)
                dve.wait_ge(s_scan, 2 * (J * k + j + 1))
                slot = (k + k // PER_SEQ + 1) * (2 * J) + 2 * j
                nc.vector.tensor_copy(carry[:, bass.ds(slot, HALVES)],
                                      hs[:, j % 2].rearrange("p (h n) -> p h n", h=HALVES)[:, :, SPAN - 1]).then_inc(s_carry, 1)

            def mixed(k, j, mid):
                dve.wait_ge(s_skip, J * k + j + 1)
                if mid or j >= 2:
                    dve.wait_ge(s_s, J * k + j - 1)
                nc.vector.scalar_tensor_tensor(out=s32[:, j % 2], in0=hs[:, j % 2], scalar=UNSCALE, in1=skip[:, j],
                                               op0=ALU.mult, op1=ALU.add).then_inc(s_sum, 1)
                dve.wait_ge(s_sum, J * k + j + 1)
                if mid:
                    dve.wait_ge(s_o_psum, k)
                nc.vector.tensor_copy(s_hi[:, j], s32[:, j % 2]).then_inc(s_s_hi, 1)
                dve.wait_ge(s_s_hi, J * k + j + 1)
                nc.vector.tensor_tensor(s_lo[:, j], s32[:, j % 2], s_hi[:, j], ALU.subtract).then_inc(s_s, 1)

            def residual_and_norms(t):
                dve.wait_ge(s_oT_psum, t + 1)
                nc.vector.tensor_tensor(x_tiles(t), bank_E[:], x_tiles(t), ALU.add).then_inc(s_x1, 1)
                dve.wait_ge(s_x1, t + 1).then_inc(s_passed, 1)
                norm_stats(2, t, lambda i: x_tiles(t, i, 1))
                for i in range(TILES):
                    nc.vector.scalar_tensor_tensor(out=u2[:, i], in0=x_tiles(t, i, 1), scalar=mean_var[2][:, i, 0:1],
                                                   in1=row_tile(scale2_rows, i // 2, t), op0=ALU.subtract,
                                                   op1=ALU.mult).then_inc(s_u2, 1)
                dve.wait_ge(s_rstd[2], t + 1)
                for i in range(TILES):
                    dve.wait_ge(s_u2, TILES * t + i + 1)
                    nc.vector.scalar_tensor_tensor(out=h2[:, i], in0=u2[:, i], scalar=rstd[2][:, i:i + 1],
                                                   in1=row_tile(shift2_rows, i // 2, t), op0=ALU.mult,
                                                   op1=ALU.add).then_inc(s_h2, 1)
                dve.wait_ge(s_h2, TILES * (t + 1))
                norm_stats(3, t, lambda i: h2[:, i])
                dve.wait_ge(s_rstd[3], t + 1)
                for i in range(TILES):
                    nc.vector.tensor_scalar(n3[:, i], h2[:, i], mean_var[3][:, i, 0:1], rstd[3][:, i:i + 1],
                                            ALU.subtract, ALU.mult).then_inc(s_n3, 1)

            def attended(t):
                dve.wait_ge(s_attn_psum, t + 1)
                dve.wait_ge(s_h2T, t + 1)
                nc.vector.scalar_tensor_tensor(out=xa[:], in0=bank_D[:], scalar=UNSCALE, in1=h2T[:], op0=ALU.mult,
                                               op1=ALU.add).then_inc(s_xa, 1)
                dve.wait_ge(s_xa, t + 1)
                nc.vector.tensor_copy(xa_hi[:], xa[:]).then_inc(s_xa_hi, 1)
                dve.wait_ge(s_xa_hi, t + 1)
                nc.vector.tensor_tensor(xa_lo[:], xa[:], xa_hi[:], ALU.subtract).then_inc(s_xa_lo, 1)

            def gates_and_rows():
                after_setup(nc.vector.memset(carry[:], 0.0))
                after_setup(nc.vector.scalar_tensor_tensor(out=magnitude[:], in0=mod[:], scalar=-1.0, in1=mod[:],
                                                           op0=ALU.mult, op1=ALU.max))
                after_setup(nc.vector.tensor_scalar(magnitude[:], magnitude[:], 0.25, None, ALU.max))
                after_setup(nc.vector.tensor_scalar(sign[:], mod[:], 0.0, 2.0, ALU.is_ge, ALU.mult))
                after_setup(nc.vector.scalar_tensor_tensor(out=sign[:], in0=sign[:], scalar=-1.0, in1=magnitude[:],
                                                           op0=ALU.add, op1=ALU.mult))
                after_setup(nc.vector.tensor_scalar(per_seq[:, T_GATE1], sign[:, 2], UNSCALE, None, ALU.mult))
                after_setup(nc.vector.tensor_scalar(per_seq[:, T_GATE1_BO], sign[:, 2], col[:, R_BO:R_BO + 1], None,
                                                    ALU.mult))
                after_setup(nc.vector.tensor_copy(per_seq[:, T_GATE2], sign[:, 5]))
                expand(T_GATE1, 3, s_tables)
                dve.wait_ge(s_mod_rows_psum, 1)
                for b in range(B):
                    both = bank_C[b // 2][:, (b % 2) * 2 * D:(b % 2 + 1) * 2 * D]
                    nc.vector.tensor_copy(shift2_rows[:, b], both[:, 0:D]).then_inc(s_rows_ready, 1)
                    nc.vector.tensor_scalar(scale2_rows[:, b], both[:, D:2 * D], 1.0, None, ALU.add).then_inc(s_rows_ready, 1)

            def step(k, front, mid, last, norm_ahead=True):
                t, u = k - 1, k - 2
                if front:
                    for j in range(J):
                        dve.wait_ge(s_xin, J * k + j + 1)
                        if mid:
                            dve.wait_ge(s_h_psum, J * k)
                        nc.vector.tensor_copy(xin_hi[:, j], xin[:, j]).then_inc(s_xin_hi, 1)
                    if not mid:
                        gates_and_rows()
                        split_lo(("wh",))
                if mid:
                    if not last:
                        dve.wait_ge(s_rows_ready, 2 * B)
                    split_expert(t, first=not last)
                if last:
                    dve.wait_ge(s_y, 2 * (u + 1))
                    nc.vector.tensor_tensor(y_lo[:], y[:], y_hi[:], ALU.subtract).then_inc(s_y_lo, 1)
                if front and norm_ahead:
                    if not mid:
                        dve.wait_ge(s_x1_in, 16 * HALVES)
                        dve.wait_ge(s_xrest_in, 16 * HALVES * (CHUNKS - 2))
                    norm1(k + 1)
                    if not mid:
                        split_lo(("wo", "wa", "wn"))
                if mid:
                    residual_and_norms(t)
                if front:
                    recur(k, 0, mid)
                if mid:
                    dve.wait_ge(s_n3T, 2 * (t + 1))
                    nc.vector.tensor_tensor(n3T_lo[:], n3T[:], n3T_hi[:], ALU.subtract).then_inc(s_n3T_lo, 1)
                if front:
                    mixed(k, 0, mid)
                if mid:
                    attended(t)
                if front:
                    recur(k, 1, mid)
                    if norm_ahead:
                        modulated_low(k + 1)
                    mixed(k, 1, mid)
                if last:
                    dve.wait_ge(s_g, u + 1)
                    for half in range(HALVES):
                        cols = slice(half * SPAN, (half + 1) * SPAN)
                        nc.vector.tensor_scalar(gated[:, cols], g[:, cols], table_col(T_GATE2, half, u), None,
                                                ALU.mult).then_inc(s_gated, 1)
                if front:
                    for j in (2, 3):
                        recur(k, j, mid)
                        mixed(k, j, mid)
                if last:
                    dve.wait_ge(s_out_psum, u + 1)
                    nc.vector.tensor_tensor(x_tiles(u), bank_E[:], x_tiles(u), ALU.add).then_inc(s_out, 1)

            def expand(first_table, count, signal):
                wide = table[:].rearrange("p (t b r) -> p t b r", t=TABLES, r=PER_SEQ)
                for r in range(PER_SEQ):
                    nc.vector.tensor_copy(wide[:, first_table:first_table + count, :, r],
                                          per_seq[:, first_table:first_table + count]).then_inc(signal, 1)

            after_setup(nc.vector.memset(ones[:], 1.0))
            dve.wait_ge(s_x0_in, 16 * HALVES)
            norm1(0, first=True)
            split_lo(("w1",))
            dve.wait_ge(s_mod_psum, 1)
            mod_psum = bank_D[:, 0:6 * B].rearrange("p (m b) -> p m b", m=6)
            nc.vector.tensor_scalar(per_seq[:, T_SCALE1], mod_psum[:, 1], 1.0, None, ALU.add).then_inc(s_setup, 1)
            nc.vector.tensor_copy(per_seq[:, T_SHIFT1], mod_psum[:, 0]).then_inc(s_setup, 1)
            setup[0] += 2
            after_setup(nc.vector.tensor_copy(mod[:], mod_psum))
            expand(T_SCALE1, 2, s_table1)
            dve.wait_ge(s_cols_psum, 1)
            nc.vector.tensor_copy(col[:], bank_E[:, P:P + ROWS]).then_inc(s_cols, 1)
            dve.wait_ge(s_cols, 1)
            nc.vector.tensor_scalar(bh_scaled[:], col[:, R_BH:R_BH + J], WSCALE, None, ALU.mult).then_inc(s_cols, 1)
            nc.vector.tensor_scalar(minus_bz[:], col[:, R_BZ:R_BZ + J], -1.0, None, ALU.mult).then_inc(s_cols, 1)
            modulated_low(0)
            split_lo(("w2", "wz"))
            run_steps(dve, step)

        @block.tensor
        def _(pe):
            def product(psum, parts, w, w_cols, block=0, first=True, final=True):
                (v_hi, v_lo), (_, w_hi, w_lo) = parts, w
                nc.tensor.matmul(psum, w_hi[:, block, w_cols], v_hi, start=first, stop=False)
                nc.tensor.matmul(psum, w_hi[:, block, w_cols], v_lo, start=False, stop=False)
                return nc.tensor.matmul(psum, w_lo[:, block, w_cols], v_hi, start=False, stop=final)

            def plane(j):
                return slice(j * P, (j + 1) * P)

            def turn(psum, src):
                for i in range(TILES):
                    last = nc.tensor.transpose(psum[:, i * P:(i + 1) * P], src(i), ident[:])
                return last

            def transpose_n1(c, first=False):
                pe.wait_ge(s_n1, TILES * (c + 1))
                if not first:
                    pe.wait_ge(s_z, 2 * J * c)
                turn(bank_B[1], lambda i: n1[:, i]).then_inc(s_n1T_psum, 1)

            def gate_plane(k, j, mid, last):
                if j < 2:
                    pe.wait_ge(s_skip, J * k + j + 3)
                else:
                    pe.wait_ge(s_z, 2 * (J * k + j - 1))
                for i in range(J):
                    if j == 0:
                        if not mid:
                            pe.wait_ge(s_w_lo, LO_BEFORE["wz"] + i + 1)
                        pe.wait_ge(s_xin_lo, J * k + i + 1)
                    mm = product(bank_B[j % 2][:], (xin_hi[:, i], xin_lo[:, i]), wz, plane(j), i, i == 0, i == J - 1)
                mm.then_inc(s_z_psum, 1)

            def hidden_plane(k, j, mid):
                if mid or j >= 2:
                    pe.wait_ge(s_b, J * k + j - 1)
                else:
                    pe.wait_ge(s_rows_ready, 2 * B)
                for i in range(J):
                    if j == 0 and not mid:
                        pe.wait_ge(s_w_lo, LO_BEFORE["wh"] + i + 1)
                    mm = product(bank_C[j % 2][:], (xin_hi[:, i], xin_lo[:, i]), wh, plane(j), i, i == 0, i == J - 1)
                mm.then_inc(s_h_psum, 1)

            def step(k, front, mid, last, norm_ahead=True):
                t, u = k - 1, k - 2
                if front:
                    pe.wait_ge(s_xm_lo, k + 1)
                    for j in range(J):
                        if not mid and j == 0:
                            pe.wait_ge(s_w_lo, LO_BEFORE["w1"] + 1)
                        if last:
                            pe.wait_ge(s_up, 2 * (J * (t - 1) + j + 1))
                        elif mid and j < 2:
                            pe.wait_ge(s_skip, J * (k - 1) + j + 1)
                        elif mid:
                            pe.wait_ge(s_z, 2 * (J * (k - 1) + j + 1))
                        product(bank_AB[j][:], (xm_hi[:], xm_lo[:]), w1, plane(j)).then_inc(s_xin_psum, 1)
                    for j in range(J):
                        if not mid and j == 0:
                            pe.wait_ge(s_w_lo, LO_BEFORE["w2"] + 1)
                        pe.wait_ge(s_xin, J * k + j + 1)
                        product(bank_AB[j][:], (xm_hi[:], xm_lo[:]), w2, plane(j)).then_inc(s_skip_psum, 1)
                if mid:
                    if not last:
                        pe.wait_ge(s_w_lo, LO_BEFORE["wn"] + 1)
                    else:
                        pe.wait_ge(s_y, 2 * t)
                    for i in range(J):
                        pe.wait_ge(s_s, J * t + i + 1)
                        mm = product(bank_D[:], (s_hi[:, i], s_lo[:, i]), wo, slice(0, D), i, i == 0, i == J - 1)
                    mm.then_inc(s_o_psum, 1)
                if front:
                    gate_plane(k, 0, mid, last)
                if mid:
                    pe.wait_ge(s_oT, 2 * (t + 1))
                    if not front:
                        pe.wait_ge(s_out, u)
                    turn(bank_E, lambda i: oT[:, i * P:(i + 1) * P]).then_inc(s_oT_psum, 1)
                if front:
                    for j in (1, 2, 3):
                        gate_plane(k, j, mid, last)
                    hidden_plane(k, 0, mid)
                if mid:
                    pe.wait_ge(s_h2, TILES * (t + 1))
                    turn(bank_E, lambda i: h2[:, i]).then_inc(s_h2T_psum, 1)
                    pe.wait_ge(s_n3, TILES * (t + 1))
                    if front:
                        pe.wait_ge(s_z, 2 * (J * (t + 1) + 3))
                    else:
                        pe.wait_ge(s_up, 2 * (J * (t - 1) + 3))
                    turn(bank_B[0], lambda i: n3[:, i]).then_inc(s_n3T_psum, 1)
                if front:
                    hidden_plane(k, 1, mid)
                if mid:
                    pe.wait_ge(s_n3T_lo, t + 1)
                    product(bank_D[:], (n3T_hi[:], n3T_lo[:]), wa, slice(0, D)).then_inc(s_attn_psum, 1)
                if front and norm_ahead:
                    transpose_n1(k + 1)
                if front:
                    hidden_plane(k, 2, mid)
                if last:
                    pe.wait_ge(s_y_lo, u + 1)
                    if mid:
                        pe.wait_ge(s_xa, t + 1)
                    product(bank_D[:], (y_hi[:], y_lo[:]), wn, slice(0, D)).then_inc(s_next_psum, 1)
                if mid:
                    pe.wait_ge(s_xa_lo, t + 1)
                    pe.wait_ge(s_e_lo, 2 * (t + 1))
                    for j in range(J):
                        if j < 2 and front:
                            pe.wait_ge(s_skip, J * (t + 1) + j + 1)
                        elif j == 3 and front and norm_ahead:
                            pe.wait_ge(s_xm, 4 * (t + 3))
                        elif j == 3 and front:
                            pe.wait_ge(s_z, 2 * J * (t + 2))
                        elif j != 2:
                            pe.wait_ge(s_up, 2 * (J * (t - 1) + j + 1))
                        product(bank_AB[j][:], (xa_hi[:], xa_lo[:]), eup, plane(j)).then_inc(s_up_psum, 1)
                if front:
                    hidden_plane(k, 3, mid)
                if last:
                    pe.wait_ge(s_gated, 2 * (u + 1))
                    if mid:
                        pe.wait_ge(s_h2T, t + 1)
                    else:
                        pe.wait_ge(s_out, u)
                    turn(bank_E, lambda i: gated[:, i * P:(i + 1) * P]).then_inc(s_out_psum, 1)
                if mid:
                    if last:
                        pe.wait_ge(s_g, u + 1)
                    for i in range(J):
                        pe.wait_ge(s_up_lo, J * t + i + 1)
                        mm = product(bank_D[:], (up_hi[:, i], up_lo[:, i]), edn, slice(0, D), i, i == 0, i == J - 1)
                    mm.then_inc(s_dn_psum, 1)

            pe.wait_ge(s_ident, 1)
            pe.wait_ge(s_cond, 16)
            nc.tensor.transpose(bank_E[:, 0:B], cond_rows[:], ident[0:B, 0:B]).then_inc(s_cond_psum, 1)
            pe.wait_ge(s_silu_c, 1)
            pe.wait_ge(s_wmod, 16)
            for m in range(6):
                mm = nc.tensor.matmul(bank_D[:, m * B:(m + 1) * B], wmod_sb[:, m * D:(m + 1) * D], silu_c[:],
                                      start=True, stop=True)
            mm.then_inc(s_mod_psum, 1)
            transpose_n1(0, first=True)
            pe.wait_ge(s_wide, B)
            for b in range(B):
                mm = nc.tensor.matmul(bank_C[b // 2][:, (b % 2) * 2 * D:(b % 2 + 1) * 2 * D], silu_c_wide[:, b],
                                      wmod_sb[:, 3 * D:5 * D], start=True, stop=True)
            mm.then_inc(s_mod_rows_psum, 1)
            pe.wait_ge(s_rows, 16 * ROW_LOADS)
            nc.tensor.transpose(bank_E[:, P:P + ROWS], param_rows[:], ident[0:ROWS, 0:ROWS]).then_inc(s_cols_psum, 1)
            run_steps(pe, step)


_INS = ["L0_attn_x", "L0_attn_W1", "L0_attn_b1", "L0_attn_W2", "L0_attn_b2", "L0_attn_Wz", "L0_attn_bz", "L0_attn_Wh",
        "L0_attn_bh", "L0_attn_Wo", "L0_attn_bo", "L0_ffn_ln_g", "L0_ffn_ln_b", "L0_ffn_attn_w", "L0_ffn_attn_b",
        "L0_ffn_w1", "L0_ffn_b1", "L0_ffn_w2", "L0_ffn_b2", "L0_ffn_next_w", "L0_ffn_next_b", "L0_c", "L0_wmod"]
_OUTS = [((4, 1024, 128), "float32")]


def kernel(**inputs):
    import numpy as _np
    import concourse.bacc as _bacc
    from concourse import mybir as _mybir
    from concourse.bass_utils import run_bass_kernel_spmd as _run

    nc = _bacc.Bacc("TRN2", target_bir_lowering=False, num_devices=1)
    arrays, args = {}, []
    for name in _INS:
        a = _np.ascontiguousarray(inputs[name])
        arrays[f"in_{name}_dram"] = a
        args.append(nc.dram_tensor(f"in_{name}_dram", a.shape, _mybir.dt.from_np(a.dtype), kind="ExternalInput").ap())
    for i, (shape, dtype) in enumerate(_OUTS):
        dt = _mybir.dt.from_np(_np.dtype(dtype))
        args.append(nc.dram_tensor(f"out_{i}_dram", shape, dt, kind="ExternalOutput").ap())
    adaln_mingru_experts(nc, *args)
    r = _run(nc, [arrays], core_ids=[0])
    got = tuple(r.results[0][f"out_{i}_dram"] for i in range(len(_OUTS)))
    return got[0]
```

```python
from contextlib import ExitStack

import concourse.bass as bass
from concourse import mybir

F32 = mybir.dt.float32
F16 = mybir.dt.float16
ALU = mybir.AluOpType
ACT = mybir.ActivationFunctionType

P = 128
WSCALE = 64.0
UNSCALE = 1.0 / WSCALE
EPS = 1e-5


def adaln_mingru_experts(nc, x, W1, b1, W2, b2, Wz, bz, Wh, bh, Wo, bo, ln_g, ln_b, attn_w, attn_b,
                         ew1, eb1, ew2, eb2, next_w, next_b, cond, wmod, out):
    B, S, D = x.shape
    EXP = W1.shape[1]
    E = ew1.shape[0]
    J = EXP // P
    HALVES = 2
    CHUNKS = E
    SPAN = B * S // (HALVES * CHUNKS)
    TILES = HALVES * SPAN // P
    N = HALVES * SPAN
    PER_SEQ = S // SPAN
    assert D == P and N == 512 and ew1.shape[2] == EXP and CHUNKS % PER_SEQ == 0 and B == 4

    R_B1, R_B2, R_BZ, R_BH = 0, J, 2 * J, 3 * J
    R_BO = 4 * J
    R_G, R_LB, R_AB, R_NB = R_BO + 1, R_BO + 2, R_BO + 3, R_BO + 4
    R_EB2 = R_BO + 5
    R_EB1 = R_EB2 + E
    ROWS = R_EB1 + E * J
    T_SCALE1, T_SHIFT1, T_GATE1, T_GATE1_BO, T_GATE2 = range(5)
    TABLES = 5
    SHIFT1, SCALE1, GATE1, SHIFT2, SCALE2, GATE2 = range(6)

    def rows(v):
        return v.rearrange("(a n) -> a n", n=P)

    def token_rows(t):
        return t.rearrange("b s d -> (b s) d").rearrange("(h k t p) d -> h k p t d", h=HALVES, k=CHUNKS, p=P)

    x_rows, out_rows = token_rows(x), token_rows(out)

    with ExitStack() as ctx:
        def sb(name, shape, dt=F32):
            return ctx.enter_context(nc.sbuf_tensor(name, shape, dt))

        def sem(name):
            return ctx.enter_context(nc.semaphore(name))

        def bank(name):
            return ctx.enter_context(nc.psum_tensor(name, [P, N], F32))

        bank_A = [bank("bank_A0"), bank("bank_A1")]
        bank_B = [bank("bank_B0"), bank("bank_B1")]
        bank_AB = bank_A + bank_B
        bank_C = [bank("bank_C0"), bank("bank_C1")]
        bank_D = bank("bank_D")
        bank_E = bank("bank_E")

        x_all = sb("x_all", [P, CHUNKS, TILES, D])
        n1 = sb("n1", [P, TILES, D])
        u2 = sb("u2", [P, TILES, D])
        h2 = sb("h2", [P, TILES, D])
        n3 = sb("n3", [P, TILES, D])
        stats = {n: sb(f"stats{n}", [P, TILES, 6]) for n in (1, 2, 3)}
        mean_var = {n: sb(f"mean_var{n}", [P, TILES, 2]) for n in (1, 2, 3)}
        var_eps = {n: sb(f"var_eps{n}", [P, TILES]) for n in (1, 2, 3)}
        rstd = {n: sb(f"rstd{n}", [P, TILES]) for n in (1, 2, 3)}
        minus_half = sb("minus_half", [P, TILES])
        table_probe = sb("table_probe", [P, 1])

        xm, xm_hi, xm_lo = sb("xm", [P, N]), sb("xm_hi", [P, N], F16), sb("xm_lo", [P, N], F16)
        xin, xin_hi, xin_lo = sb("xin", [P, J, N]), sb("xin_hi", [P, J, N], F16), sb("xin_lo", [P, J, N], F16)
        skip = sb("skip", [P, J, N])
        z = sb("z", [P, J, N])
        a = sb("a", [P, J, N])
        bb = sb("bb", [P, 2, N])
        hs = sb("hs", [P, 2, N])
        carry = sb("carry", [P, (CHUNKS // PER_SEQ) * (PER_SEQ + 1) * 2 * J])
        s32, s_hi, s_lo = sb("s32", [P, 2, N]), sb("s_hi", [P, J, N], F16), sb("s_lo", [P, J, N], F16)
        oT = sb("oT", [P, N])
        h2T = sb("h2T", [P, N])
        n3T, n3T_hi, n3T_lo = sb("n3T", [P, N]), sb("n3T_hi", [P, N], F16), sb("n3T_lo", [P, N], F16)
        xa, xa_hi, xa_lo = sb("xa", [P, N]), sb("xa_hi", [P, N], F16), sb("xa_lo", [P, N], F16)
        up, up_hi, up_lo = sb("up", [P, J, N]), sb("up_hi", [P, J, N], F16), sb("up_lo", [P, J, N], F16)
        y, y_hi, y_lo = sb("y", [P, N]), sb("y_hi", [P, N], F16), sb("y_lo", [P, N], F16)
        g = sb("g", [P, N])
        gated = sb("gated", [P, N])

        def weight(name, blocks, cols):
            return (sb(f"{name}_raw", [P, blocks, cols]), sb(f"{name}_hi", [P, blocks, cols], F16),
                    sb(f"{name}_lo", [P, blocks, cols], F16))

        w1, w2 = weight("w1", 1, EXP), weight("w2", 1, EXP)
        wz, wh = weight("wz", J, EXP), weight("wh", J, EXP)
        wo, wa, wn = weight("wo", J, D), weight("wa", 1, D), weight("wn", 1, D)
        eup, edn = weight("eup", 1, EXP), weight("edn", J, D)

        cond_rows = sb("cond_rows", [B, P])
        param_rows = sb("param_rows", [ROWS, P])
        col = sb("col", [P, ROWS])
        wmod_sb = sb("wmod_sb", [P, 6 * D])
        ident = sb("ident", [P, P])
        ones = sb("ones", [P, P])
        zeros = sb("zeros", [P, N], F16)
        silu_c = sb("silu_c", [P, B])
        silu_c_wide = sb("silu_c_wide", [P, B, P])
        wide_hi, wide_lo = sb("wide_hi", [P, B, P], F16), sb("wide_lo", [P, B, P], F16)
        wmod2_hi, wmod2_lo = sb("wmod2_hi", [P, 2 * D], F16), sb("wmod2_lo", [P, 2 * D], F16)
        mod = sb("mod", [P, 2, B])
        magnitude, sign = sb("magnitude", [P, 2, B]), sb("sign", [P, 2, B])
        per_seq = sb("per_seq", [P, TABLES, B])
        table = sb("table", [P, TABLES * HALVES * CHUNKS])
        shift2_rows = sb("shift2_rows", [P, B, D])
        scale2_rows = sb("scale2_rows", [P, B, D])
        bh_scaled = sb("bh_scaled", [P, J])
        minus_bz = sb("minus_bz", [P, J])

        s_cond, s_rows, s_wmod_norm1, s_wmod = sem("s_cond"), sem("s_rows"), sem("s_wmod_norm1"), sem("s_wmod")
        s_x0_in, s_x1_in, s_xrest_in = sem("s_x0_in"), sem("s_x1_in"), sem("s_xrest_in")
        s_raw = {n: sem(f"s_raw_{n}") for n in ("w1", "w2", "wz", "wh", "wo", "wa", "wn")}
        s_eup_raw, s_edn_raw = sem("s_eup_raw"), sem("s_edn_raw")
        s_stored = sem("s_stored")
        s_ident0, s_ident, s_half, s_zeros = sem("s_ident0"), sem("s_ident"), sem("s_half"), sem("s_zeros")
        s_setup = sem("s_setup")
        s_cond_psum, s_silu_c, s_mod_psum = sem("s_cond_psum"), sem("s_silu_c"), sem("s_mod_psum")
        s_cols_psum, s_mod_rows_psum = sem("s_cols_psum"), sem("s_mod_rows_psum")
        s_wide_parts = sem("s_wide_parts")
        s_wide, s_table1, s_cols, s_tables = sem("s_wide"), sem("s_table1"), sem("s_cols"), sem("s_tables")
        s_wz_hi, s_rows_ready = sem("s_wz_hi"), sem("s_rows_ready")
        s_w_hi, s_w_lo = sem("s_w_hi"), sem("s_w_lo")
        s_stats = {n: sem(f"s_stats{n}") for n in (1, 2, 3)}
        s_mv = {n: sem(f"s_mv{n}") for n in (1, 2, 3)}
        s_var = {n: sem(f"s_var{n}") for n in (1, 2, 3)}
        s_rstd = {n: sem(f"s_rstd{n}") for n in (1, 2, 3)}
        s_n1, s_u2, s_h2, s_n3 = sem("s_n1"), sem("s_u2"), sem("s_h2"), sem("s_n3")
        s_passed = sem("s_passed")
        s_xm_hi_first = sem("s_xm_hi_first")
        s_xm_lo_first = sem("s_xm_lo_first")
        s_n1T_psum, s_xm, s_xm_lo = sem("s_n1T_psum"), sem("s_xm"), sem("s_xm_lo")
        s_xin_psum, s_xin, s_xin_hi, s_xin_lo = sem("s_xin_psum"), sem("s_xin"), sem("s_xin_hi"), sem("s_xin_lo")
        s_skip_psum, s_skip = sem("s_skip_psum"), sem("s_skip")
        s_z_psum, s_z = sem("s_z_psum"), sem("s_z")
        s_h_psum, s_b, s_scan, s_carry = sem("s_h_psum"), sem("s_b"), sem("s_scan"), sem("s_carry")
        s_sum, s_s_hi, s_s = sem("s_sum"), sem("s_s_hi"), sem("s_s")
        s_e_hi, s_e_lo = sem("s_e_hi"), sem("s_e_lo")
        s_o_psum, s_oT, s_oT_psum, s_x1 = sem("s_o_psum"), sem("s_oT"), sem("s_oT_psum"), sem("s_x1")
        s_h2T_psum, s_h2T, s_n3T_psum, s_n3T, s_n3T_lo = (
            sem("s_h2T_psum"), sem("s_h2T"), sem("s_n3T_psum"), sem("s_n3T"), sem("s_n3T_lo"))
        s_attn_psum, s_xa, s_xa_hi, s_xa_lo = sem("s_attn_psum"), sem("s_xa"), sem("s_xa_hi"), sem("s_xa_lo")
        s_up_psum, s_up, s_up_lo = sem("s_up_psum"), sem("s_up"), sem("s_up_lo")
        s_dn_psum, s_y, s_y_lo = sem("s_dn_psum"), sem("s_y"), sem("s_y_lo")
        s_up_closing, s_up_hi_closing = sem("s_up_closing"), sem("s_up_hi_closing")
        s_up_lo_dve, s_up_lo_pool = sem("s_up_lo_dve"), sem("s_up_lo_pool")
        s_next_psum, s_g, s_gated, s_out_psum, s_out = (
            sem("s_next_psum"), sem("s_g"), sem("s_gated"), sem("s_out_psum"), sem("s_out"))

        W_ORDER = [("w1", w1, 1), ("w2", w2, 1)] + [("wz", wz, J), ("wh", wh, J), ("wo", wo, 1), ("wa", wa, 1), ("wn", wn, 1)]
        LO_BEFORE, HI_BEFORE, n, m = {}, {}, 0, 0
        for name, _, blocks in W_ORDER:
            LO_BEFORE[name], HI_BEFORE[name] = n, m
            n += blocks
            m += 0 if name == "wz" else blocks

        ROW_LOADS = 11
        XM_FIRST, XM_STEPS = HALVES, 2 * HALVES

        def table_col(which, half, c):
            return table[:, bass.ds(which * HALVES * CHUNKS + half * CHUNKS + c, 1)]

        def row_tile(t, half, c):
            return t[:].rearrange("p b d -> p (b d)")[:, bass.ds((c // PER_SEQ + 2 * half) * D, D)]

        def x_tiles(c, i=0, count=TILES):
            return x_all[:].rearrange("p c t d -> p (c t d)")[:, bass.ds(c * (TILES * D) + i * D, count * D)]

        def carry_cols(c, j, half, count):
            return carry[:, bass.ds((c + c // PER_SEQ) * (2 * J) + 2 * j + half, count)]

        def weight_blocks(w, blocks):
            flat = [t[:].rearrange("p b n -> p (b n)") for t in w]
            width = flat[0].shape[1] // blocks
            return [[t[:, i * width:(i + 1) * width] for t in flat] for i in range(blocks)]

        def run_steps(eng, step):
            step(0, mid=False, last=False)
            step(1, mid=True, last=False)
            with eng.Fori(2, CHUNKS - 1) as k:
                step(k, mid=True, last=True)
            step(CHUNKS - 1, mid=True, last=True, final=True)

        L = CHUNKS - 1
        PARTS = (0, 1)

        def section(part):
            if part is None:
                return range(TILES), slice(0, N), 0
            per = TILES // HALVES
            return range(part * per, (part + 1) * per), slice(part * SPAN, (part + 1) * SPAN), part

        bank_o, bank_prod, bank_out = (bank_C[0], bank_E), (bank_D, bank_C[0]), (bank_E, bank_C[0])
        bank_n3T, bank_up = (bank_B[0], bank_B[1]), (bank_A, bank_B)
        POOL_PLANES = range(1, J, 2)
        DVE_PLANES = range(0, J, 2)

        block = ctx.enter_context(nc.Block())

        @block.sync
        def _(sp):
            def load_x(c, loaded):
                for half in range(HALVES):
                    tiles = slice(half * TILES // 2, (half + 1) * TILES // 2)
                    sp.dma_start(x_all[:, c, tiles], x_rows[half, c]).then_inc(loaded, 16)

            load_x(0, s_x0_in)
            sp.dma_start(cond_rows[:], cond).then_inc(s_cond, 16)
            sp.dma_start(wmod_sb[:, 0:2 * D], wmod[:, 0:2 * D]).then_inc(s_wmod_norm1, 16)
            sp.dma_start(w1[0][:, 0], W1).then_inc(s_raw["w1"], 16)
            sp.dma_start(wmod_sb[:, 2 * D:], wmod[:, 2 * D:]).then_inc(s_wmod, 16)
            sp.dma_start(wz[0][:], Wz.rearrange("(b p) n -> p b n", p=P)).then_inc(s_raw["wz"], 16)
            for at, v in ((R_B1, b1), (R_B2, b2), (R_BZ, bz), (R_BH, bh), (R_BO, bo), (R_G, ln_g), (R_LB, ln_b),
                          (R_AB, attn_b), (R_NB, next_b)):
                count = v.shape[0] // P
                sp.dma_start(param_rows[at:at + count, :], rows(v)).then_inc(s_rows, 16)
            sp.dma_start(param_rows[R_EB2:R_EB2 + E, :], eb2).then_inc(s_rows, 16)
            sp.dma_start(param_rows[R_EB1:R_EB1 + E * J, :], eb1.rearrange("e (j n) -> (e j) n", n=P)).then_inc(s_rows, 16)
            sp.dma_start(w2[0][:, 0], W2).then_inc(s_raw["w2"], 16)
            sp.dma_start(wh[0][:], Wh.rearrange("(b p) n -> p b n", p=P)).then_inc(s_raw["wh"], 16)
            load_x(1, s_x1_in)
            sp.dma_start(wo[0][:], Wo.rearrange("(b p) n -> p b n", p=P)).then_inc(s_raw["wo"], 16)
            sp.dma_start(wa[0][:, 0], attn_w).then_inc(s_raw["wa"], 16)
            sp.dma_start(wn[0][:, 0], next_w).then_inc(s_raw["wn"], 16)
            sp.dma_start(eup[0][:, 0], ew1[0]).then_inc(s_eup_raw, 16)
            sp.dma_start(edn[0][:], ew2[0].rearrange("(b p) n -> p b n", p=P)).then_inc(s_edn_raw, 16)
            for c in range(2, CHUNKS):
                load_x(c, s_xrest_in)

            def load_expert(e):
                sp.wait_ge(s_e_lo, 2 * e)
                sp.dma_start(eup[0][:, 0], ew1.rearrange("e p n -> (e p) n")[bass.ds(e * P, P), :]).then_inc(s_eup_raw, 16)
                sp.dma_start(edn[0][:], ew2.rearrange("e (b p) n -> e p b n", p=P)[e]).then_inc(s_edn_raw, 16)

            def store(u):
                for half in range(HALVES):
                    sp.wait_ge(s_out, u + 1 + (half if isinstance(u, int) and u == L else 0))
                    rows_out = x_tiles(u, half * TILES // 2, TILES // 2).rearrange("p (t d) -> p t d", d=D)
                    sp.dma_start(out_rows[half, u], rows_out).then_inc(s_stored, 16)

            load_expert(1)
            with sp.Fori(2, CHUNKS) as e:
                load_expert(e)
                store(e - 2)
            store(L - 1)
            store(L)
            sp.wait_ge(s_stored, 16 * HALVES * CHUNKS)

        @block.gpsimd
        def _(pool):
            nc.gpsimd.memset(ident[:], 0.0).then_inc(s_ident0, 1)
            nc.gpsimd.memset(minus_half[:], -0.5).then_inc(s_half, 1)
            pool.wait_ge(s_ident0, 1)
            nc.gpsimd.affine_select(out=ident[:], in_=ident[:], compare_op=ALU.not_equal, fill=1.0, base=0,
                                    pattern=[[-1, P]], channel_multiplier=1).then_inc(s_ident, 1)

            def rsqrt(n, c):
                pool.wait_ge(s_var[n], c + 1)
                nc.gpsimd.tensor_tensor(rstd[n][:], var_eps[n][:], minus_half[:], ALU.pow).then_inc(s_rstd[n], 1)

            def step(k, mid, last, final=False):
                t = k - 1
                for j in range(J):
                    pool.wait_ge(s_xin_hi, J * k + j + 1)
                    nc.gpsimd.tensor_tensor(xin_lo[:, j], xin[:, j], xin_hi[:, j], ALU.subtract).then_inc(s_xin_lo, 1)
                if not final:
                    rsqrt(1, k + 1)
                if mid:
                    rsqrt(2, t)
                    rsqrt(3, t)
                    if final:
                        for j in range(J - 1):
                            pool.wait_ge(s_s_hi, J * k + j + 1)
                            nc.gpsimd.tensor_tensor(s_lo[:, j], s32[:, j % 2], s_hi[:, j], ALU.subtract).then_inc(s_s, 1)
                    for j in range(J - 1 if final else J):
                        expanded_low(t, j)

            def expanded_low(t, j):
                pool.wait_ge(s_up, 2 * (J * t + j + 1))
                nc.gpsimd.tensor_tensor(up_lo[:, j], up[:, j], up_hi[:, j], ALU.subtract).then_inc(s_up_lo, 1)

            def closing():
                rsqrt(2, L)
                expanded_low(L - 1, J - 1)
                rsqrt(3, L)
                pool.wait_ge(s_y, 2 * L)
                nc.gpsimd.tensor_tensor(y_lo[:], y[:], y_hi[:], ALU.subtract).then_inc(s_y_lo, 1)
                for part in PARTS:
                    cols = section(part)[1]
                    for j in POOL_PLANES:
                        pool.wait_ge(s_up_hi_closing, J * part + j + 1)
                        nc.gpsimd.tensor_tensor(up_lo[:, j, cols], up[:, j, cols], up_hi[:, j, cols],
                                                ALU.subtract).then_inc(s_up_lo_pool, 1)

            pool.wait_ge(s_half, 1)
            rsqrt(1, 0)
            pool.wait_ge(s_raw["wz"], 16)
            for raw, hi, _ in weight_blocks(wz, J):
                nc.gpsimd.tensor_scalar(hi, raw, WSCALE, 1.0, ALU.mult, ALU.mult).then_inc(s_wz_hi, 1)
            run_steps(pool, step)
            closing()

        @block.scalar
        def _(act):
            def load_table(func):
                nc.scalar.activation(table_probe[:], minus_half[:, 0:1], func)

            act.wait_ge(s_half, 1)
            load_table(ACT.Silu)
            act.wait_ge(s_cond_psum, 1)
            nc.scalar.activation(silu_c[:], bank_E[:, 0:B], ACT.Silu).then_inc(s_silu_c, 1)

            def split_hi(names):
                for name, w, blocks in W_ORDER:
                    if name in names:
                        act.wait_ge(s_raw[name], 16)
                        for raw, hi, _ in weight_blocks(w, blocks):
                            nc.scalar.activation(hi, raw, ACT.Copy, scale=WSCALE).then_inc(s_w_hi, 1)

            def modulate(c, first=False):
                act.wait_ge(s_n1T_psum, c + 1)
                if not first:
                    act.wait_ge(s_xm_lo, c)
                    act.wait_ge(s_skip_psum, J * c)
                for dst in (xm,) if first else (xm, xm_hi):
                    for half in range(HALVES):
                        cols = slice(half * SPAN, (half + 1) * SPAN)
                        nc.scalar.activation(dst[:, cols], bank_B[1][:, cols], ACT.Identity,
                                             scale=table_col(T_SCALE1, half, c),
                                             bias=table_col(T_SHIFT1, half, c)).then_inc(s_xm, 1)

            def expert_result(u, product, part=None):
                _, cols, p = section(part)
                act.wait_ge(s_dn_psum, u + p + 1)
                for dst in (y, y_hi):
                    nc.scalar.activation(dst[:, cols], product[:, cols], ACT.Identity, scale=UNSCALE,
                                         bias=col[:, bass.ds(R_EB2 + u, 1)]).then_inc(s_y, 1)

            def gated_mix(t, later):
                if later:
                    act.wait_ge(s_oT_psum, t)
                act.wait_ge(s_o_psum, t + 1)
                for half in range(HALVES):
                    cols = slice(half * SPAN, (half + 1) * SPAN)
                    nc.scalar.activation(oT[:, cols], bank_D[:, cols], ACT.Identity,
                                         scale=table_col(T_GATE1, half, t),
                                         bias=table_col(T_GATE1_BO, half, t)).then_inc(s_oT, 1)

            def turned_h2(t, later):
                act.wait_ge(s_h2T_psum, t + 1)
                if later:
                    act.wait_ge(s_xa, t)
                nc.scalar.activation(h2T[:], bank_E[:], ACT.Identity, bias=col[:, R_AB:R_AB + 1]).then_inc(s_h2T, 1)

            def turned_n3(t, later, n3T_bank, part=None):
                _, cols, p = section(part)
                act.wait_ge(s_n3T_psum, t + p + 1)
                if later and p == 0:
                    act.wait_ge(s_n3T_lo, t)
                    act.wait_ge(s_attn_psum, t)
                for dst in (n3T, n3T_hi):
                    nc.scalar.activation(dst[:, cols], n3T_bank[:, cols], ACT.Identity, scale=col[:, R_G:R_G + 1],
                                         bias=col[:, R_LB:R_LB + 1]).then_inc(s_n3T, 1)

            def next_gelu(u, product, part=None):
                _, cols, p = section(part)
                act.wait_ge(s_next_psum, u + p + 1)
                nc.scalar.activation(g[:, cols], product[:, cols], ACT.Gelu, scale=UNSCALE,
                                     bias=col[:, R_NB:R_NB + 1]).then_inc(s_g, 1)

            def step(k, mid, last, final=False):
                t, u = k - 1, k - 2
                load_table(ACT.Silu)
                for j in range(J):
                    act.wait_ge(s_xin_psum, J * k + j + 1)
                    if mid:
                        act.wait_ge(s_xin_lo, J * (k - 1) + j + 1)
                    nc.scalar.activation(xin[:, j], bank_AB[j][:], ACT.Silu, scale=UNSCALE,
                                         bias=col[:, R_B1 + j:R_B1 + j + 1]).then_inc(s_xin, 1)
                if mid and not last:
                    for j in range(J):
                        act.wait_ge(s_xin, J * k + j + 1)
                        act.wait_ge(s_h_psum, J * k)
                        nc.scalar.activation(xin_hi[:, j], xin[:, j], ACT.Copy).then_inc(s_xin_hi, 1)
                if last:
                    expert_result(u, bank_D)
                for j in range(J):
                    act.wait_ge(s_skip_psum, J * k + j + 1)
                    if mid:
                        act.wait_ge(s_sum, J * (k - 1) + j + 1)
                    nc.scalar.activation(skip[:, j], bank_AB[j][:], ACT.Silu, scale=UNSCALE,
                                         bias=col[:, R_B2 + j:R_B2 + j + 1]).then_inc(s_skip, 1)
                if not mid:
                    split_hi(("wh",))
                if mid:
                    if not last:
                        act.wait_ge(s_tables, PER_SEQ)
                    gated_mix(t, last)
                for j in range(J):
                    act.wait_ge(s_z_psum, J * k + j + 1)
                    if mid:
                        act.wait_ge(s_scan, 2 * (J * (k - 1) + j + 1))
                    nc.scalar.activation(z[:, j], bank_B[j % 2][:], ACT.Sigmoid, scale=UNSCALE,
                                         bias=col[:, R_BZ + j:R_BZ + j + 1]).then_inc(s_z, 1)
                    nc.scalar.activation(a[:, j], bank_B[j % 2][:], ACT.Sigmoid, scale=-UNSCALE,
                                         bias=minus_bz[:, j:j + 1]).then_inc(s_z, 1)
                if not mid:
                    split_hi(("wo", "wa", "wn"))
                if mid:
                    turned_h2(t, last)
                    turned_n3(t, last, bank_B[0])
                if not final:
                    modulate(k + 1)
                if final:
                    for j in range(2):
                        mixed_high(k, j)
                if last:
                    next_gelu(u, bank_D)
                if final:
                    mixed_high(k, 2)
                    gate2(u)
                if mid:
                    for j in range(J // 2 if final else J):
                        expanded(t, j, last)

            def mixed_high(k, j):
                act.wait_ge(s_sum, J * k + j + 1)
                act.wait_ge(s_o_psum, k)
                nc.scalar.activation(s_hi[:, j], s32[:, j % 2], ACT.Copy).then_inc(s_s_hi, 1)

            def expanded(t, j, later):
                act.wait_ge(s_up_psum, J * t + j + 1)
                if later:
                    act.wait_ge(s_up_lo, J * (t - 1) + j + 1)
                    act.wait_ge(s_dn_psum, t)
                for dst in (up, up_hi):
                    nc.scalar.activation(dst[:, j], bank_AB[j][:], ACT.Gelu, scale=UNSCALE,
                                         bias=col[:, bass.ds(R_EB1 + J * t + j, 1)]).then_inc(s_up, 1)

            def gate2(u):
                act.wait_ge(s_g, u + 1)
                for half in range(HALVES):
                    cols = slice(half * SPAN, (half + 1) * SPAN)
                    nc.scalar.activation(gated[:, cols], g[:, cols], ACT.Identity,
                                         scale=table_col(T_GATE2, half, u)).then_inc(s_gated, 1)

            def closing():
                gated_mix(L, True)
                for j in range(J // 2, J):
                    expanded(L - 1, j, True)
                expert_result(L - 1, bank_C[1])
                turned_h2(L, True)
                for part in PARTS:
                    turned_n3(L, True, bank_n3T[part], part)
                next_gelu(L - 1, bank_C[1])
                act.wait_ge(s_out, L - 1)
                gate2(L - 1)
                act.wait_ge(s_up_lo, J * L)
                act.wait_ge(s_dn_psum, L)
                for part in PARTS:
                    _, cols, p = section(part)
                    for j in range(J):
                        act.wait_ge(s_up_psum, J * (L + p) + 2 * (j // 2) + 2)
                        nc.scalar.activation(up[:, j, cols], bank_up[part][j // 2][:, (j % 2) * SPAN:(j % 2 + 1) * SPAN],
                                             ACT.Gelu, scale=UNSCALE,
                                             bias=col[:, R_EB1 + J * L + j:R_EB1 + J * L + j + 1]).then_inc(s_up_closing, 1)
                for part in PARTS:
                    expert_result(L, bank_prod[part], part)
                for part in PARTS:
                    next_gelu(L, bank_prod[part], part)

            split_hi(("w1",))
            act.wait_ge(s_table1, PER_SEQ)
            modulate(0, first=True)
            split_hi(("w2",))
            act.wait_ge(s_cols, 3)
            run_steps(act, step)
            closing()

        @block.vector
        def _(dve):
            setup = [0]

            def after_setup(ins):
                setup[0] += 1
                ins.then_inc(s_setup, 1)
                dve.wait_ge(s_setup, setup[0])

            def norm_stats(n, c, tile):
                for i in range(TILES):
                    nc.vector.bn_stats(stats[n][:, i], tile(i)).then_inc(s_stats[n], 1)
                dve.wait_ge(s_stats[n], TILES * (c + 1)).then_inc(s_passed, 1)
                for i in range(TILES):
                    nc.vector.bn_aggr(mean_var[n][:, i], stats[n][:, i]).then_inc(s_mv[n], 1)
                dve.wait_ge(s_mv[n], TILES * (c + 1))
                nc.vector.tensor_scalar(var_eps[n][:], mean_var[n][:, :, 1], EPS, None, ALU.add).then_inc(s_var[n], 1)

            def norm1(c):
                norm_stats(1, c, lambda i: x_tiles(c, i, 1))
                normalised1(c)

            def normalised1(c, first=False):
                dve.wait_ge(s_rstd[1], c + 1)
                if not first:
                    dve.wait_ge(s_n1T_psum, c)
                for i in range(TILES):
                    nc.vector.tensor_scalar(n1[:, i], x_tiles(c, i, 1), mean_var[1][:, i, 0:1], rstd[1][:, i:i + 1],
                                            ALU.subtract, ALU.mult).then_inc(s_n1, 1)

            def modulated_low(c):
                dve.wait_ge(s_xm, XM_STEPS * c + XM_FIRST)
                nc.vector.tensor_tensor(xm_lo[:], xm[:], xm_hi[:], ALU.subtract).then_inc(s_xm_lo, 1)

            def modulated_first():
                for half in range(HALVES):
                    cols = slice(half * SPAN, (half + 1) * SPAN)
                    dve.wait_ge(s_xm, half + 1)
                    nc.vector.tensor_copy(xm_hi[:, cols], xm[:, cols]).then_inc(s_xm_hi_first, 1)
                for half in range(HALVES):
                    cols = slice(half * SPAN, (half + 1) * SPAN)
                    dve.wait_ge(s_xm_hi_first, half + 1)
                    nc.vector.tensor_tensor(xm_lo[:, cols], xm[:, cols], xm_hi[:, cols],
                                            ALU.subtract).then_inc(s_xm_lo if half == HALVES - 1 else s_xm_lo_first, 1)

            def split_lo(names):
                for name, w, blocks in W_ORDER:
                    if name in names:
                        for i, (raw, hi, lo) in enumerate(weight_blocks(w, blocks)):
                            if name == "wz":
                                dve.wait_ge(s_wz_hi, i + 1)
                            else:
                                dve.wait_ge(s_w_hi, HI_BEFORE[name] + i + 1)
                            nc.vector.scalar_tensor_tensor(out=lo, in0=raw, scalar=WSCALE, in1=hi, op0=ALU.mult,
                                                           op1=ALU.subtract).then_inc(s_w_lo, 1)

            def split_expert(t, which):
                w, loaded = ((eup, s_eup_raw), (edn, s_edn_raw))[which]
                raw, hi, lo = weight_blocks(w, 1)[0]
                dve.wait_ge(loaded, 16 * (t + 1))
                nc.vector.tensor_scalar(hi, raw, WSCALE, None, ALU.mult).then_inc(s_e_hi, 1)
                dve.wait_ge(s_e_hi, 2 * t + which + 1)
                nc.vector.scalar_tensor_tensor(out=lo, in0=raw, scalar=WSCALE, in1=hi, op0=ALU.mult,
                                               op1=ALU.subtract).then_inc(s_e_lo, 1)

            def recur(k, j, mid):
                driven(k, j, mid)
                scanned(k, j, mid)
                dve.wait_ge(s_scan, 2 * (J * k + j + 1))
                slot = (k + k // PER_SEQ + 1) * (2 * J) + 2 * j
                nc.vector.tensor_copy(carry[:, bass.ds(slot, HALVES)],
                                      hs[:, j % 2].rearrange("p (h n) -> p h n", h=HALVES)[:, :, SPAN - 1]).then_inc(s_carry, 1)

            def driven(k, j, mid):
                dve.wait_ge(s_h_psum, J * k + j + 1)
                dve.wait_ge(s_z, 2 * (J * k + j + 1))
                if mid or j >= 2:
                    dve.wait_ge(s_sum, J * k + j - 1)
                nc.vector.scalar_tensor_tensor(out=bb[:, j % 2], in0=bank_C[j % 2][:], scalar=bh_scaled[:, j:j + 1],
                                               in1=z[:, j], op0=ALU.add, op1=ALU.mult).then_inc(s_b, 1)

            def scanned(k, j, mid):
                dve.wait_ge(s_b, J * k + j + 1)
                if mid:
                    dve.wait_ge(s_carry, J * (k - 1) + j + 1)
                for half in range(HALVES):
                    cols = slice(half * SPAN, (half + 1) * SPAN)
                    nc.vector.tensor_tensor_scan(hs[:, j % 2, cols], a[:, j, cols], bb[:, j % 2, cols],
                                                 carry_cols(k, j, half, 1), ALU.mult, ALU.add).then_inc(s_scan, 1)

            def summed(k, j, mid):
                dve.wait_ge(s_scan, 2 * (J * k + j + 1))
                dve.wait_ge(s_skip, J * k + j + 1)
                if mid or j >= 2:
                    dve.wait_ge(s_s, J * k + j - 1)
                nc.vector.scalar_tensor_tensor(out=s32[:, j % 2], in0=hs[:, j % 2], scalar=UNSCALE, in1=skip[:, j],
                                               op0=ALU.mult, op1=ALU.add).then_inc(s_sum, 1)

            def mixed(k, j, mid):
                summed(k, j, mid)
                dve.wait_ge(s_sum, J * k + j + 1)
                if mid:
                    dve.wait_ge(s_o_psum, k)
                nc.vector.tensor_copy(s_hi[:, j], s32[:, j % 2]).then_inc(s_s_hi, 1)
                dve.wait_ge(s_s_hi, J * k + j + 1)
                nc.vector.tensor_tensor(s_lo[:, j], s32[:, j % 2], s_hi[:, j], ALU.subtract).then_inc(s_s, 1)

            def last_mixed(k):
                j, done = J - 1, J * k + J - 1
                halves = [slice(half * SPAN, (half + 1) * SPAN) for half in range(HALVES)]
                dve.wait_ge(s_skip, done + 1)
                dve.wait_ge(s_s, done - 1)
                for half, cols in enumerate(halves):
                    dve.wait_ge(s_scan, 2 * done + half + 1)
                    nc.vector.scalar_tensor_tensor(out=s32[:, j % 2, cols], in0=hs[:, j % 2, cols], scalar=UNSCALE,
                                                   in1=skip[:, j, cols], op0=ALU.mult, op1=ALU.add).then_inc(s_sum, 1)
                dve.wait_ge(s_s, done)
                for half, cols in enumerate(halves):
                    dve.wait_ge(s_sum, done + half + 1)
                    nc.vector.tensor_copy(s_hi[:, j, cols], s32[:, j % 2, cols]).then_inc(s_s_hi, 1)
                for half, cols in enumerate(halves):
                    dve.wait_ge(s_s_hi, done + half + 1)
                    nc.vector.tensor_tensor(s_lo[:, j, cols], s32[:, j % 2, cols], s_hi[:, j, cols],
                                            ALU.subtract).then_inc(s_s, 1)

            def residual1(t, psum, part=None):
                tiles, cols, p = section(part)
                x_part = x_tiles(t, tiles.start, len(tiles))
                dve.wait_ge(s_oT_psum, t + p + 1)
                nc.vector.tensor_tensor(x_part, psum[:, cols], x_part, ALU.add).then_inc(s_x1, 1)

            def centred(t, parts=1):
                dve.wait_ge(s_x1, t + parts).then_inc(s_passed, 1)
                norm_stats(2, t, lambda i: x_tiles(t, i, 1))
                for i in range(TILES):
                    nc.vector.scalar_tensor_tensor(out=u2[:, i], in0=x_tiles(t, i, 1), scalar=mean_var[2][:, i, 0:1],
                                                   in1=row_tile(scale2_rows, i // 2, t), op0=ALU.subtract,
                                                   op1=ALU.mult).then_inc(s_u2, 1)

            def modulated2(t):
                dve.wait_ge(s_rstd[2], t + 1)
                for i in range(TILES):
                    dve.wait_ge(s_u2, TILES * t + i + 1)
                    nc.vector.scalar_tensor_tensor(out=h2[:, i], in0=u2[:, i], scalar=rstd[2][:, i:i + 1],
                                                   in1=row_tile(shift2_rows, i // 2, t), op0=ALU.mult,
                                                   op1=ALU.add).then_inc(s_h2, 1)
                dve.wait_ge(s_h2, TILES * (t + 1))
                norm_stats(3, t, lambda i: h2[:, i])

            def normalised3(t):
                dve.wait_ge(s_rstd[3], t + 1)
                for i in range(TILES):
                    nc.vector.tensor_scalar(n3[:, i], h2[:, i], mean_var[3][:, i, 0:1], rstd[3][:, i:i + 1],
                                            ALU.subtract, ALU.mult).then_inc(s_n3, 1)

            def norm3_low(t, part=None):
                _, cols, p = section(part)
                dve.wait_ge(s_n3T, 2 * (t + p + 1))
                nc.vector.tensor_tensor(n3T_lo[:, cols], n3T[:, cols], n3T_hi[:, cols], ALU.subtract).then_inc(s_n3T_lo, 1)

            def attended(t, product, part=None):
                _, cols, p = section(part)
                dve.wait_ge(s_attn_psum, t + p + 1)
                dve.wait_ge(s_h2T, t + 1)
                nc.vector.scalar_tensor_tensor(out=xa[:, cols], in0=product[:, cols], scalar=UNSCALE, in1=h2T[:, cols],
                                               op0=ALU.mult, op1=ALU.add).then_inc(s_xa, 1)
                dve.wait_ge(s_xa, t + p + 1)
                nc.vector.tensor_copy(xa_hi[:, cols], xa[:, cols]).then_inc(s_xa_hi, 1)
                dve.wait_ge(s_xa_hi, t + p + 1)
                nc.vector.tensor_tensor(xa_lo[:, cols], xa[:, cols], xa_hi[:, cols], ALU.subtract).then_inc(s_xa_lo, 1)

            def result_low(u, part=None):
                _, cols, p = section(part)
                dve.wait_ge(s_y, 2 * (u + p + 1))
                nc.vector.tensor_tensor(y_lo[:, cols], y[:, cols], y_hi[:, cols], ALU.subtract).then_inc(s_y_lo, 1)

            def gate2(u, halves=range(HALVES)):
                for half in halves:
                    cols = slice(half * SPAN, (half + 1) * SPAN)
                    nc.vector.tensor_scalar(gated[:, cols], g[:, cols], table_col(T_GATE2, half, u), None,
                                            ALU.mult).then_inc(s_gated, 1)

            def residual2(u, psum, part=None):
                tiles, cols, p = section(part)
                x_part = x_tiles(u, tiles.start, len(tiles))
                dve.wait_ge(s_out_psum, u + p + 1)
                nc.vector.tensor_tensor(x_part, psum[:, cols], x_part, ALU.add).then_inc(s_out, 1)

            def mod_psum(m):
                return bank_D[:, m * B:(m + 1) * B]

            def gates_and_rows():
                after_setup(nc.vector.memset(carry[:], 0.0))
                dve.wait_ge(s_mod_psum, 2)
                for i, m in enumerate((GATE1, GATE2)):
                    after_setup(nc.vector.tensor_copy(mod[:, i], mod_psum(m)))
                after_setup(nc.vector.scalar_tensor_tensor(out=magnitude[:], in0=mod[:], scalar=-1.0, in1=mod[:],
                                                           op0=ALU.mult, op1=ALU.max))
                after_setup(nc.vector.tensor_scalar(magnitude[:], magnitude[:], 0.25, None, ALU.max))
                after_setup(nc.vector.tensor_scalar(sign[:], mod[:], 0.0, 2.0, ALU.is_ge, ALU.mult))
                after_setup(nc.vector.scalar_tensor_tensor(out=sign[:], in0=sign[:], scalar=-1.0, in1=magnitude[:],
                                                           op0=ALU.add, op1=ALU.mult))
                after_setup(nc.vector.tensor_scalar(per_seq[:, T_GATE1], sign[:, 0], UNSCALE, None, ALU.mult))
                after_setup(nc.vector.tensor_scalar(per_seq[:, T_GATE1_BO], sign[:, 0], col[:, R_BO:R_BO + 1], None,
                                                    ALU.mult))
                after_setup(nc.vector.tensor_copy(per_seq[:, T_GATE2], sign[:, 1]))
                expand(T_GATE1, 3, s_tables)
                dve.wait_ge(s_mod_rows_psum, 2)
                for b in range(B):
                    both = bank_C[b // 2][:, (b % 2) * 2 * D:(b % 2 + 1) * 2 * D]
                    nc.vector.tensor_scalar(shift2_rows[:, b], both[:, 0:D], UNSCALE * UNSCALE, None,
                                            ALU.mult).then_inc(s_rows_ready, 1)
                    nc.vector.tensor_scalar(scale2_rows[:, b], both[:, D:2 * D], UNSCALE * UNSCALE, 1.0, ALU.mult,
                                            ALU.add).then_inc(s_rows_ready, 1)

            def step(k, mid, last, final=False):
                t, u = k - 1, k - 2
                for j in range(J) if last or not mid else ():
                    dve.wait_ge(s_xin, J * k + j + 1)
                    if mid:
                        dve.wait_ge(s_h_psum, J * k)
                    nc.vector.tensor_copy(xin_hi[:, j], xin[:, j]).then_inc(s_xin_hi, 1)
                if not mid:
                    split_lo(("wz",))
                if not mid:
                    gates_and_rows()
                    split_lo(("wh",))
                if mid:
                    if last:
                        dve.wait_ge(s_dn_psum, t)
                    else:
                        dve.wait_ge(s_rows_ready, 2 * B)
                    split_expert(t, 0)
                    split_expert(t, 1)
                if last:
                    result_low(u)
                if not final:
                    if not mid:
                        dve.wait_ge(s_x1_in, 16 * HALVES)
                        dve.wait_ge(s_xrest_in, 16 * HALVES * (CHUNKS - 2))
                    norm1(k + 1)
                    if not mid:
                        split_lo(("wo", "wa", "wn"))
                if mid:
                    residual1(t, bank_E)
                    centred(t)
                    modulated2(t)
                    normalised3(t)
                if final:
                    driven(k, 0, mid)
                    scanned(k, 0, mid)
                    norm3_low(t)
                    summed(k, 0, mid)
                    driven(k, 1, mid)
                    attended(t, bank_D)
                    scanned(k, 1, mid)
                    driven(k, 2, mid)
                    summed(k, 1, mid)
                    scanned(k, 2, mid)
                    driven(k, 3, mid)
                    summed(k, 2, mid)
                    scanned(k, 3, mid)
                    last_mixed(k)
                    return
                recur(k, 0, mid)
                if mid:
                    norm3_low(t)
                mixed(k, 0, mid)
                if mid:
                    attended(t, bank_D)
                recur(k, 1, mid)
                modulated_low(k + 1)
                mixed(k, 1, mid)
                if last:
                    dve.wait_ge(s_g, u + 1)
                    gate2(u)
                for j in (2, 3):
                    recur(k, j, mid)
                    mixed(k, j, mid)
                if last:
                    residual2(u, bank_E)

            def closing():
                residual2(L - 2, bank_E)
                for part in PARTS:
                    residual1(L, bank_o[part], part)
                centred(L, parts=len(PARTS))
                modulated2(L)
                dve.wait_ge(s_up_psum, J * L)
                split_expert(L, 0)
                normalised3(L)
                dve.wait_ge(s_dn_psum, L)
                split_expert(L, 1)
                for part in PARTS:
                    norm3_low(L, part)
                for part in PARTS:
                    attended(L, bank_prod[part], part)
                for part in PARTS:
                    _, cols, p = section(part)
                    for j in range(J):
                        dve.wait_ge(s_up_closing, J * p + j + 1)
                        nc.vector.tensor_copy(up_hi[:, j, cols], up[:, j, cols]).then_inc(s_up_hi_closing, 1)
                        if j - 1 in DVE_PLANES:
                            up_low(part, j - 1)
                for part in PARTS:
                    result_low(L, part)
                    if part == 0:
                        residual2(L - 1, bank_C[1])
                for part in PARTS:
                    dve.wait_ge(s_g, L + part + 1)
                    gate2(L, (part,))
                for part in PARTS:
                    residual2(L, bank_out[part], part)

            def up_low(part, j):
                cols = section(part)[1]
                dve.wait_ge(s_up_hi_closing, J * part + j + 1)
                nc.vector.tensor_tensor(up_lo[:, j, cols], up[:, j, cols], up_hi[:, j, cols],
                                        ALU.subtract).then_inc(s_up_lo_dve, 1)

            def expand(first_table, count, signal):
                wide = table[:].rearrange("p (t b r) -> p t b r", t=TABLES, r=PER_SEQ)
                for r in range(PER_SEQ):
                    nc.vector.tensor_copy(wide[:, first_table:first_table + count, :, r],
                                          per_seq[:, first_table:first_table + count]).then_inc(signal, 1)

            nc.vector.memset(zeros[:], 0.0).then_inc(s_zeros, 1)
            after_setup(nc.vector.memset(ones[:], 1.0))
            dve.wait_ge(s_x0_in, 16 * HALVES)
            norm_stats(1, 0, lambda i: x_tiles(0, i, 1))
            dve.wait_ge(s_mod_psum, 1)
            nc.vector.tensor_scalar(per_seq[:, T_SCALE1], mod_psum(SCALE1), 1.0, None, ALU.add).then_inc(s_setup, 1)
            nc.vector.tensor_copy(per_seq[:, T_SHIFT1], mod_psum(SHIFT1)).then_inc(s_setup, 1)
            setup[0] += 2
            dve.wait_ge(s_setup, setup[0])
            expand(T_SCALE1, 2, s_table1)
            normalised1(0, first=True)
            dve.wait_ge(s_silu_c, 1)
            for b in range(B):
                nc.vector.tensor_scalar(silu_c_wide[:, b], ones[:], silu_c[:, b:b + 1], None, ALU.mult).then_inc(s_wide, 1)
            split_lo(("w1",))
            modulated_first()
            wmod2 = wmod_sb[:, 3 * D:5 * D]
            dve.wait_ge(s_wide, B)
            nc.vector.tensor_scalar(wide_hi[:], silu_c_wide[:], WSCALE, None, ALU.mult).then_inc(s_wide_parts, 1)
            dve.wait_ge(s_wmod, 16)
            nc.vector.tensor_scalar(wmod2_hi[:], wmod2, WSCALE, None, ALU.mult).then_inc(s_wide_parts, 1)
            dve.wait_ge(s_wide_parts, 2)
            nc.vector.scalar_tensor_tensor(out=wide_lo[:], in0=silu_c_wide[:], scalar=WSCALE, in1=wide_hi[:],
                                           op0=ALU.mult, op1=ALU.subtract).then_inc(s_wide_parts, 1)
            nc.vector.scalar_tensor_tensor(out=wmod2_lo[:], in0=wmod2, scalar=WSCALE, in1=wmod2_hi[:],
                                           op0=ALU.mult, op1=ALU.subtract).then_inc(s_wide_parts, 1)
            dve.wait_ge(s_cols_psum, 1)
            nc.vector.tensor_copy(col[:], bank_E[:, P:P + ROWS]).then_inc(s_cols, 1)
            dve.wait_ge(s_cols, 1)
            nc.vector.tensor_scalar(bh_scaled[:], col[:, R_BH:R_BH + J], WSCALE, None, ALU.mult).then_inc(s_cols, 1)
            nc.vector.tensor_scalar(minus_bz[:], col[:, R_BZ:R_BZ + J], -1.0, None, ALU.mult).then_inc(s_cols, 1)
            split_lo(("w2",))
            run_steps(dve, step)
            closing()

        @block.tensor
        def _(pe):
            def product(psum, parts, w, w_cols, block=0, first=True, final=True, low=None):
                (v_hi, v_lo), (_, w_hi, w_lo) = parts, w
                nc.tensor.matmul(psum, w_hi[:, block, w_cols], v_hi, start=first, stop=False)
                nc.tensor.matmul(psum, w_lo[:, block, w_cols], v_hi, start=False, stop=False)
                if low is not None:
                    pe.wait_ge(*low)
                return nc.tensor.matmul(psum, w_hi[:, block, w_cols], v_lo, start=False, stop=final)

            def plane(j):
                return slice(j * P, (j + 1) * P)

            def turn(psum, src, part=None):
                for i in section(part)[0]:
                    last = nc.tensor.transpose(psum[:, i * P:(i + 1) * P], src(i), ident[:])
                return last

            def transpose_n1(c, first=False):
                if not first:
                    pe.wait_ge(s_z, 2 * J * c)
                for i in range(TILES):
                    pe.wait_ge(s_n1, TILES * c + i + 1)
                    last = nc.tensor.transpose(bank_B[1][:, i * P:(i + 1) * P], n1[:, i], ident[:])
                last.then_inc(s_n1T_psum, 1)

            def gate_plane(k, j, mid):
                if j < 2:
                    pe.wait_ge(s_skip, J * k + j + 3)
                else:
                    pe.wait_ge(s_z, 2 * (J * k + j - 1))
                if j == 0:
                    for i in range(J):
                        if not mid:
                            pe.wait_ge(s_w_lo, LO_BEFORE["wz"] + i + 1)
                        pe.wait_ge(s_xin_hi, J * k + i + 1)
                        for w in wz[1:]:
                            nc.tensor.matmul(bank_B[0][:], w[:, i, plane(0)], xin_hi[:, i], start=i == 0 and w is wz[1],
                                             stop=False)
                    for i in range(J):
                        pe.wait_ge(s_xin_lo, J * k + i + 1)
                        mm = nc.tensor.matmul(bank_B[0][:], wz[1][:, i, plane(0)], xin_lo[:, i], start=False,
                                              stop=i == J - 1)
                else:
                    for i in range(J):
                        mm = product(bank_B[j % 2][:], (xin_hi[:, i], xin_lo[:, i]), wz, plane(j), i, i == 0, i == J - 1)
                mm.then_inc(s_z_psum, 1)

            def hidden_plane(k, j, mid):
                if mid or j >= 2:
                    pe.wait_ge(s_b, J * k + j - 1)
                else:
                    pe.wait_ge(s_rows_ready, 2 * B)
                for i in range(J):
                    if j == 0 and not mid:
                        pe.wait_ge(s_w_lo, LO_BEFORE["wh"] + i + 1)
                    mm = product(bank_C[j % 2][:], (xin_hi[:, i], xin_lo[:, i]), wh, plane(j), i, i == 0, i == J - 1)
                mm.then_inc(s_h_psum, 1)

            def output_projection(t, halved=False):
                for i in range(J):
                    made = J * t + i + 1 + (1 if halved and i == J - 1 else 0)
                    pe.wait_ge(s_s_hi, made)
                    mm = product(bank_D[:], (s_hi[:, i], s_lo[:, i]), wo, slice(0, D), i, i == 0, i == J - 1,
                                 low=(s_s, made))
                mm.then_inc(s_o_psum, 1)

            def turn_h2(t):
                pe.wait_ge(s_h2, TILES * (t + 1))
                turn(bank_E, lambda i: h2[:, i]).then_inc(s_h2T_psum, 1)

            def turn_n3(t, psum, part=None):
                pe.wait_ge(s_n3, TILES * t + section(part)[0].stop)
                turn(psum, lambda i: n3[:, i], part).then_inc(s_n3T_psum, 1)

            def attention_product(t, psum, part=None):
                _, cols, p = section(part)
                pe.wait_ge(s_n3T, 2 * (t + p + 1))
                product(psum[:, cols], (n3T_hi[:, cols], n3T_lo[:, cols]), wa, slice(0, D),
                        low=(s_n3T_lo, t + p + 1)).then_inc(s_attn_psum, 1)

            def next_product(u, psum, part=None):
                _, cols, p = section(part)
                pe.wait_ge(s_y, 2 * (u + p + 1))
                product(psum[:, cols], (y_hi[:, cols], y_lo[:, cols]), wn, slice(0, D),
                        low=(s_y_lo, u + p + 1)).then_inc(s_next_psum, 1)

            def expert_down(t, psum, planes=range(J)):
                pe.wait_ge(s_e_lo, 2 * t + 2)
                for i in planes:
                    pe.wait_ge(s_up, 2 * (J * t + i + 1))
                    mm = product(psum[:], (up_hi[:, i], up_lo[:, i]), edn, slice(0, D), i, i == 0, i == J - 1,
                                 low=(s_up_lo, J * t + i + 1))
                return mm

            def last_expert_down(psum, part):
                cols = section(part)[1]
                pe.wait_ge(s_e_lo, 2 * L + 2)
                for i in range(J):
                    made, planes = (s_up_lo_dve, DVE_PLANES) if i in DVE_PLANES else (s_up_lo_pool, POOL_PLANES)
                    pe.wait_ge(s_up_hi_closing, J * part + i + 1)
                    mm = product(psum[:, cols], (up_hi[:, i, cols], up_lo[:, i, cols]), edn, slice(0, D), i, i == 0,
                                 i == J - 1, low=(made, len(planes) * part + planes.index(i) + 1))
                mm.then_inc(s_dn_psum, 1)

            def turn_gated(u, psum, part=None):
                pe.wait_ge(s_gated, 2 * u + (2 if part is None else part + 1))
                turn(psum, lambda i: gated[:, i * P:(i + 1) * P], part).then_inc(s_out_psum, 1)

            def step(k, mid, last, final=False):
                t, u = k - 1, k - 2
                if mid:
                    pe.wait_ge(s_xm_lo, k + 1)
                for j in range(J):
                    if not mid and j == 0:
                        pe.wait_ge(s_w_lo, LO_BEFORE["w1"] + 1)
                    if last:
                        pe.wait_ge(s_up, 2 * (J * (t - 1) + j + 1))
                    elif mid and j < 2:
                        pe.wait_ge(s_skip, J * (k - 1) + j + 1)
                    elif mid:
                        pe.wait_ge(s_z, 2 * (J * (k - 1) + j + 1))
                    if not mid and j == 0:
                        pe.wait_ge(s_xm_hi_first, HALVES)
                        product(bank_AB[j][:], (xm_hi[:], xm_lo[:]), w1, plane(j), low=(s_xm_lo, 1)).then_inc(s_xin_psum, 1)
                        parameter_columns()
                    else:
                        product(bank_AB[j][:], (xm_hi[:], xm_lo[:]), w1, plane(j)).then_inc(s_xin_psum, 1)
                if not mid:
                    modulation((GATE1, GATE2), s_wmod)
                    pe.wait_ge(s_wide_parts, 4)
                    mod_rows(0)
                    mod_rows(1)
                for j in range(J):
                    if not mid and j == 0:
                        pe.wait_ge(s_w_lo, LO_BEFORE["w2"] + 1)
                    pe.wait_ge(s_xin, J * k + j + 1)
                    product(bank_AB[j][:], (xm_hi[:], xm_lo[:]), w2, plane(j)).then_inc(s_skip_psum, 1)
                if mid:
                    if not last:
                        pe.wait_ge(s_w_lo, LO_BEFORE["wn"] + 1)
                    else:
                        pe.wait_ge(s_y, 2 * t)
                    output_projection(t)
                gate_plane(k, 0, mid)
                if mid:
                    pe.wait_ge(s_oT, 2 * (t + 1))
                    turn(bank_E, lambda i: oT[:, i * P:(i + 1) * P]).then_inc(s_oT_psum, 1)
                for j in (1, 2, 3):
                    gate_plane(k, j, mid)
                hidden_plane(k, 0, mid)
                if mid:
                    turn_h2(t)
                    pe.wait_ge(s_z, 2 * (J * (t + 1) + 3))
                    turn_n3(t, bank_B[0])
                hidden_plane(k, 1, mid)
                if mid:
                    attention_product(t, bank_D)
                if not final:
                    transpose_n1(k + 1)
                hidden_plane(k, 2, mid)
                if final:
                    hidden_plane(k, 3, mid)
                if last:
                    pe.wait_ge(s_xa, t + 1)
                    next_product(u, bank_D)
                if mid:
                    pe.wait_ge(s_xa_hi, t + 1)
                    pe.wait_ge(s_e_lo, 2 * t + 1)
                    for j in range(J):
                        if j < 2:
                            pe.wait_ge(s_skip, J * (t + 1) + j + 1)
                        elif j == 3 and not final:
                            pe.wait_ge(s_xm, XM_STEPS * (t + 2) + XM_FIRST)
                        elif j == 3:
                            pe.wait_ge(s_z, 2 * J * (t + 2))
                        product(bank_AB[j][:], (xa_hi[:], xa_lo[:]), eup, plane(j),
                                low=(s_xa_lo, t + 1)).then_inc(s_up_psum, 1)
                if not final:
                    hidden_plane(k, 3, mid)
                    if last:
                        pe.wait_ge(s_h2T, t + 1)
                        turn_gated(u, bank_E)
                    if mid:
                        if last:
                            pe.wait_ge(s_g, u + 1)
                        expert_down(t, bank_D).then_inc(s_dn_psum, 1)

            def keep_busy(bank, count):
                for _ in range(count):
                    nc.tensor.matmul(bank[:], zeros[:, 0:P], zeros[:], start=True, stop=True)

            def closing():
                pe.wait_ge(s_g, L - 1)
                output_projection(L, halved=True)
                pe.wait_ge(s_h2T, L)
                turn_gated(L - 2, bank_E)
                pe.wait_ge(s_b, J * (L + 1))
                expert_down(L - 1, bank_C[1], range(1))
                for part in PARTS:
                    pe.wait_ge(s_oT, 2 * L + part + 1)
                    if part == 1:
                        pe.wait_ge(s_out, L - 1)
                    turn(bank_o[part], lambda i: oT[:, i * P:(i + 1) * P], part).then_inc(s_oT_psum, 1)
                expert_down(L - 1, bank_C[1], range(1, J)).then_inc(s_dn_psum, 1)
                pe.wait_ge(s_up, 2 * J * L)
                keep_busy(bank_A[0], 2)
                turn_h2(L)
                keep_busy(bank_A[0], 3)
                for part in PARTS:
                    turn_n3(L, bank_n3T[part], part)
                next_product(L - 1, bank_C[1])
                for part in PARTS:
                    attention_product(L, bank_prod[part], part)
                for part in PARTS:
                    _, cols, p = section(part)
                    pe.wait_ge(s_xa_hi, L + p + 1)
                    pe.wait_ge(s_e_lo, 2 * L + 1)
                    for j in range(J):
                        product(bank_up[part][j // 2][:, (j % 2) * SPAN:(j % 2 + 1) * SPAN],
                                (xa_hi[:, cols], xa_lo[:, cols]), eup, plane(j),
                                low=(s_xa_lo, L + p + 1)).then_inc(s_up_psum, 1)
                turn_gated(L - 1, bank_C[1])
                for part in PARTS:
                    last_expert_down(bank_prod[part], part)
                for part in PARTS:
                    next_product(L, bank_prod[part], part)
                for part in PARTS:
                    turn_gated(L, bank_out[part], part)

            def parameter_columns():
                pe.wait_ge(s_rows, 16 * ROW_LOADS)
                nc.tensor.transpose(bank_E[:, P:P + ROWS], param_rows[:], ident[0:ROWS, 0:ROWS]).then_inc(s_cols_psum, 1)

            def mod_rows(pair):
                for b in (2 * pair, 2 * pair + 1):
                    psum = bank_C[pair][:, (b % 2) * 2 * D:(b % 2 + 1) * 2 * D]
                    nc.tensor.matmul(psum, wide_hi[:, b], wmod2_hi[:], start=True, stop=False)
                    nc.tensor.matmul(psum, wide_hi[:, b], wmod2_lo[:], start=False, stop=False)
                    mm = nc.tensor.matmul(psum, wide_lo[:, b], wmod2_hi[:], start=False, stop=True)
                mm.then_inc(s_mod_rows_psum, 1)

            def modulation(kinds, loaded):
                pe.wait_ge(loaded, 16)
                for m in kinds:
                    mm = nc.tensor.matmul(bank_D[:, m * B:(m + 1) * B], wmod_sb[:, m * D:(m + 1) * D], silu_c[:],
                                          start=True, stop=True)
                mm.then_inc(s_mod_psum, 1)

            pe.wait_ge(s_ident, 1)
            pe.wait_ge(s_cond, 16)
            nc.tensor.transpose(bank_E[:, 0:B], cond_rows[:], ident[0:B, 0:B]).then_inc(s_cond_psum, 1)
            pe.wait_ge(s_silu_c, 1)
            modulation((SHIFT1, SCALE1), s_wmod_norm1)
            pe.wait_ge(s_zeros, 1)
            keep_busy(bank_C[0], 3)
            transpose_n1(0, first=True)
            keep_busy(bank_C[0], 4)
            run_steps(pe, step)
            closing()


_INS = ["L0_attn_x", "L0_attn_W1", "L0_attn_b1", "L0_attn_W2", "L0_attn_b2", "L0_attn_Wz", "L0_attn_bz", "L0_attn_Wh",
        "L0_attn_bh", "L0_attn_Wo", "L0_attn_bo", "L0_ffn_ln_g", "L0_ffn_ln_b", "L0_ffn_attn_w", "L0_ffn_attn_b",
        "L0_ffn_w1", "L0_ffn_b1", "L0_ffn_w2", "L0_ffn_b2", "L0_ffn_next_w", "L0_ffn_next_b", "L0_c", "L0_wmod"]
_OUTS = [((4, 1024, 128), "float32")]


def kernel(**inputs):
    import numpy as _np
    import concourse.bacc as _bacc
    from concourse import mybir as _mybir
    from concourse.bass_utils import run_bass_kernel_spmd as _run

    nc = _bacc.Bacc("TRN2", target_bir_lowering=False, num_devices=1)
    arrays, args = {}, []
    for name in _INS:
        a = _np.ascontiguousarray(inputs[name])
        arrays[f"in_{name}_dram"] = a
        args.append(nc.dram_tensor(f"in_{name}_dram", a.shape, _mybir.dt.from_np(a.dtype), kind="ExternalInput").ap())
    for i, (shape, dtype) in enumerate(_OUTS):
        dt = _mybir.dt.from_np(_np.dtype(dtype))
        args.append(nc.dram_tensor(f"out_{i}_dram", shape, dt, kind="ExternalOutput").ap())
    adaln_mingru_experts(nc, *args)
    r = _run(nc, [arrays], core_ids=[0])
    got = tuple(r.results[0][f"out_{i}_dram"] for i in range(len(_OUTS)))
    return got[0]
```
